# Optimizing a Trainium2 kernel written in Bass

```python
import numpy as np
import jax
import jax.numpy as jnp

def _softmax(x, axis=-1):
    return jax.nn.softmax(x, axis=axis)

def _gelu(x):
    return jax.nn.gelu(x, approximate=True)

def _silu(x):
    return jax.nn.silu(x)

def _sigmoid(x):
    return jax.nn.sigmoid(x)

def _layernorm(x, axis=-1, eps=1e-05):
    m = jnp.mean(x, axis=axis, keepdims=True)
    v = jnp.var(x, axis=axis, keepdims=True)
    return (x - m) / jnp.sqrt(v + eps)

def _scatter_add(tgt, idx, src, axis=0):
    return tgt.at[idx].add(src)

def _segment_sum(src, seg, n):
    return jax.ops.segment_sum(src, seg, n)
kernel_name = 'mk_flamingo_gated_d4_seqx_r8_6bf2c6'

def setup_inputs(seed: int=0):
    np.random.seed(seed)
    _w = jnp.asarray

    def _rec_inputs():
        import jax
        import jax.numpy as jnp
        _rk = jax.random.key(seed)
        x = -1.394e-06 + 0.9999 * jax.random.normal(jax.random.fold_in(_rk, 1), (128, 64, 128), jnp.float32)
        _lenS = 64 - jax.random.randint(jax.random.fold_in(_rk, 7), (128,), 0, max(1, 64 // 4) + 1, jnp.int32)
        _lenS2 = 64 - jax.random.randint(jax.random.fold_in(_rk, 8), (128,), 0, max(1, 64 // 4) + 1, jnp.int32)
        _ctx_1024P = jax.random.normal(jax.random.fold_in(_rk, 11), (128, 16, 128), jnp.float32)
        _ctx_1024c = jax.random.dirichlet(jax.random.fold_in(_rk, 511), 0.3 * jnp.ones((16,), jnp.float32), (128, 64))
        _ctx_1024t = jnp.einsum('bsk,bkd->bsd', _ctx_1024c, _ctx_1024P)
        _ctx_1024t = _ctx_1024t * jax.lax.rsqrt(jnp.mean(jnp.square(_ctx_1024t)) + 1e-12) * 0.953939
        ctx_1024 = -0.000292821 + 1.00034 * (_ctx_1024t + 0.3 * jax.random.normal(jax.random.fold_in(_rk, 611), (128, 64, 128), jnp.float32))
        _validS = jnp.arange(64)[None, :] < _lenS[:, None]
        _validS2 = jnp.arange(64)[None, :] < _lenS2[:, None]
        _causal = jnp.tril(jnp.ones((64, 64), dtype=bool))
        mask_Bx1xSxS2_if1 = jnp.where(jnp.ones((128, 1, 64, 64), dtype=bool), 1, 0).astype(jnp.int32)
        mask_BxS2_ik0 = jnp.where(jnp.broadcast_to(_validS2[:, :], (128, 64)), 0, 1).astype(jnp.int32)
        mask_Bx1xSxS2_ik1 = jnp.where(jnp.broadcast_to(_validS2[:, None, None, :], (128, 1, 64, 64)), 1, 0).astype(jnp.int32)
        _g = jax.random.normal(jax.random.fold_in(_rk, 9001), (2, 4), jnp.float32)
        _g = jnp.sign(_g) * jnp.maximum(jnp.abs(_g), 1.0) + (_g == 0) * 1.0
        g_xattn = _g[0]
        g_ffn = _g[1]
        return (x, ctx_1024, mask_Bx1xSxS2_if1, mask_BxS2_ik0, mask_Bx1xSxS2_ik1, g_xattn, g_ffn)
    x, ctx_1024, mask_Bx1xSxS2_if1, mask_BxS2_ik0, mask_Bx1xSxS2_ik1, g_xattn, g_ffn = _rec_inputs()

    def _L0_xattn_setup():
        import jax, jax.numpy as jnp
        import numpy as np
        D_MODEL = 128
        HEADS = 16
        HEAD_DIM = D_MODEL // HEADS
        B, S = (2, 256)
        key0 = jax.random.key(seed)
        ks = jax.random.split(key0, 8)
        inp = {'key': jax.random.normal(ks[0], (B, S, D_MODEL), dtype=jnp.float32), 'query': jax.random.normal(ks[1], (B, S, D_MODEL), dtype=jnp.float32), 'value': jax.random.normal(ks[2], (B, S, D_MODEL), dtype=jnp.float32), 'mask': jnp.ones((B, 1, S, S), dtype=jnp.int32), 'Wq': jax.random.normal(ks[3], (D_MODEL, D_MODEL), dtype=jnp.float32) * 0.02, 'Wk': jax.random.normal(ks[4], (D_MODEL, D_MODEL), dtype=jnp.float32) * 0.02, 'Wv': jax.random.normal(ks[5], (D_MODEL, D_MODEL), dtype=jnp.float32) * 0.02, 'Wo': jax.random.normal(ks[6], (D_MODEL, D_MODEL), dtype=jnp.float32) * 0.02, 'bo': jax.random.normal(ks[7], (D_MODEL,), dtype=jnp.float32) * 0.02}
        return inp
    _L0_xattn_all = _L0_xattn_setup()
    _L0_xattn_in = {k: v for k, v in _L0_xattn_all.items() if k in ('Wq', 'Wk', 'Wv', 'Wo', 'bo')}
    del _L0_xattn_all

    def _L0_ffn_setup():
        import jax, jax.numpy as jnp
        import numpy as np
        import math
        B, S, H = (8, 512, 128)
        E, I, K = (8, 256, 2)
        CAP_FACTOR = 1.0

        def _router(x, expert_embeddings):
            dot = jnp.einsum('bsh,eh->bse', x, expert_embeddings)
            n = dot.shape[0] * dot.shape[1]
            dot2 = dot.reshape(n, E)
            vals, idx = jax.lax.top_k(dot2, K)
            rows = jnp.arange(n)[:, None]
            masked = jnp.full_like(dot2, -jnp.inf).at[rows, idx].set(vals)
            return jax.nn.softmax(masked, axis=-1)
        key = jax.random.key(seed)
        k1, k2, k3, k4 = jax.random.split(key, 4)

        def kaiming(k, shape):
            bound = math.sqrt(3.0 / shape[-1])
            return jax.random.uniform(k, shape, jnp.float32, -bound, bound)
        x = jax.random.normal(k1, (B, S, H), jnp.float32)
        expert_embeddings = kaiming(k2, (E, H))
        first_linear = kaiming(k3, (E, I, H))
        second_linear = kaiming(k4, (E, H, I))
        return {'x': x, 'expert_embeddings': expert_embeddings, 'first_linear': first_linear, 'second_linear': second_linear}
    _L0_ffn_all = _L0_ffn_setup()
    _L0_ffn_in = {k: v for k, v in _L0_ffn_all.items() if k in ('expert_embeddings', 'first_linear', 'second_linear')}
    del _L0_ffn_all

    def _L1_xattn_setup():
        import jax, jax.numpy as jnp
        import numpy as np
        B, S, D, H = (2, 256, 128, 16)
        HD = D // H
        SCALE = HD ** (-0.5)
        NEG = -1000000000.0
        key = jax.random.key(seed)
        ks = jax.random.split(key, 7)
        w_std = 1.0 / np.sqrt(D)
        return {'query': jax.random.normal(ks[0], (B, S, D), dtype=jnp.float32), 'key': jax.random.normal(ks[1], (B, S, D), dtype=jnp.float32), 'value': jax.random.normal(ks[2], (B, S, D), dtype=jnp.float32), 'Wq': jax.random.normal(ks[3], (D, D), dtype=jnp.float32) * w_std, 'Wk': jax.random.normal(ks[4], (D, D), dtype=jnp.float32) * w_std, 'Wv': jax.random.normal(ks[5], (D, D), dtype=jnp.float32) * w_std, 'Wo': jax.random.normal(ks[6], (D, D), dtype=jnp.float32) * w_std}
    _L1_xattn_all = _L1_xattn_setup()
    _L1_xattn_in = {k: v for k, v in _L1_xattn_all.items() if k in ('Wq', 'Wk', 'Wv', 'Wo')}
    del _L1_xattn_all

    def _L1_ffn_setup():
        import jax, jax.numpy as jnp
        import numpy as np
        B, S, D = (2, 256, 128)
        I = 64
        E = 16
        TOP_K = 2

        def _mlp(x, wg, wu, wd):
            return jnp.einsum('bsi,id->bsd', jax.nn.silu(x @ wg) * (x @ wu), wd)
        key = jax.random.key(seed)
        ks = jax.random.split(key, 10)
        sc_d = 1.0 / np.sqrt(D)
        sc_i = 1.0 / np.sqrt(I)
        return {'x': jax.random.normal(ks[0], (B, S, D), dtype=jnp.float32), 'gate_w': jax.random.normal(ks[1], (D, E), dtype=jnp.float32) * sc_d, 'gate_b': jnp.zeros((E,), dtype=jnp.float32), 'shared_wg': jax.random.normal(ks[2], (D, I), dtype=jnp.float32) * sc_d, 'shared_wu': jax.random.normal(ks[3], (D, I), dtype=jnp.float32) * sc_d, 'shared_wd': jax.random.normal(ks[4], (I, D), dtype=jnp.float32) * sc_i, 'experts_wg': jax.random.normal(ks[5], (E, D, I), dtype=jnp.float32) * sc_d, 'experts_wu': jax.random.normal(ks[6], (E, D, I), dtype=jnp.float32) * sc_d, 'experts_wd': jax.random.normal(ks[7], (E, I, D), dtype=jnp.float32) * sc_i}
    _L1_ffn_all = _L1_ffn_setup()
    _L1_ffn_in = {k: v for k, v in _L1_ffn_all.items() if k in ('gate_w', 'gate_b', 'shared_wg', 'shared_wu', 'shared_wd', 'experts_wg', 'experts_wu', 'experts_wd')}
    del _L1_ffn_all

    def _L2_xattn_setup():
        import jax, jax.numpy as jnp
        import numpy as np
        B, S, D, H = (2, 256, 128, 16)
        HD = D // H

        def _split_heads(x):
            Bb, Ss, Dd = x.shape
            return x.reshape(Bb, Ss, H, HD).transpose(0, 2, 1, 3)
        key0 = jax.random.key(seed)
        ks = jax.random.split(key0, 12)
        scale = 1.0 / np.sqrt(D)
        inp = {'query': jax.random.normal(ks[0], (B, S, D), jnp.float32), 'key': jax.random.normal(ks[1], (B, S, D), jnp.float32), 'value': jax.random.normal(ks[2], (B, S, D), jnp.float32), 'mask': jax.random.randint(ks[3], (B, S), 0, 2, jnp.int32), 'Wq': jax.random.normal(ks[4], (D, D), jnp.float32) * scale, 'bq': jnp.zeros((D,), jnp.float32), 'Wk': jax.random.normal(ks[5], (D, D), jnp.float32) * scale, 'bk': jnp.zeros((D,), jnp.float32), 'Wv': jax.random.normal(ks[6], (D, D), jnp.float32) * scale, 'bv': jnp.zeros((D,), jnp.float32), 'Wo': jax.random.normal(ks[7], (D, D), jnp.float32) * scale, 'bo': jnp.zeros((D,), jnp.float32)}
        return inp
    _L2_xattn_all = _L2_xattn_setup()
    _L2_xattn_in = {k: v for k, v in _L2_xattn_all.items() if k in ('Wq', 'bq', 'Wk', 'bk', 'Wv', 'bv', 'Wo', 'bo')}
    del _L2_xattn_all

    def _L2_ffn_setup():
        import jax, jax.numpy as jnp
        import numpy as np
        DIM = 128
        INTER = 256
        E = 8
        TOPK = 2
        ROUTE_SCALE = 1.0

        def _mlp(x, w1, w2, w3):
            h = jax.nn.silu(x @ w1.T) * (x @ w3.T)
            return h @ w2.T
        key = jax.random.key(seed)
        ks = jax.random.split(key, 10)
        s_in = 0.02
        return {'x': jax.random.normal(ks[0], (4, 256, DIM), dtype=jnp.float32), 'gate_w': jax.random.normal(ks[1], (E, DIM), dtype=jnp.float32) * s_in, 'gate_bias': jax.random.normal(ks[2], (E,), dtype=jnp.float32) * 0.01, 'w1': jax.random.normal(ks[3], (E, INTER, DIM), dtype=jnp.float32) * s_in, 'w2': jax.random.normal(ks[4], (E, DIM, INTER), dtype=jnp.float32) * s_in, 'w3': jax.random.normal(ks[5], (E, INTER, DIM), dtype=jnp.float32) * s_in, 'sw1': jax.random.normal(ks[6], (INTER, DIM), dtype=jnp.float32) * s_in, 'sw2': jax.random.normal(ks[7], (DIM, INTER), dtype=jnp.float32) * s_in, 'sw3': jax.random.normal(ks[8], (INTER, DIM), dtype=jnp.float32) * s_in}
    _L2_ffn_all = _L2_ffn_setup()
    _L2_ffn_in = {k: v for k, v in _L2_ffn_all.items() if k in ('gate_w', 'gate_bias', 'w1', 'w2', 'w3', 'sw1', 'sw2', 'sw3')}
    del _L2_ffn_all

    def _L3_xattn_setup():
        import jax, jax.numpy as jnp
        import numpy as np
        N, S, E, H = (4, 256, 128, 16)
        D = E // H
        key = jax.random.key(seed)
        ks = jax.random.split(key, 12)
        s = 1.0 / np.sqrt(E)
        inp = {'value': jax.random.normal(ks[0], (N, S, E), jnp.float32), 'key': jax.random.normal(ks[1], (N, S, E), jnp.float32), 'query': jax.random.normal(ks[2], (N, S, E), jnp.float32), 'mask': jax.random.randint(ks[3], (N, 1, S, S), 0, 2, dtype=jnp.int32), 'Wv': jax.random.normal(ks[4], (E, E), jnp.float32) * s, 'bv': jax.random.normal(ks[5], (E,), jnp.float32) * s, 'Wk': jax.random.normal(ks[6], (E, E), jnp.float32) * s, 'bk': jax.random.normal(ks[7], (E,), jnp.float32) * s, 'Wq': jax.random.normal(ks[8], (E, E), jnp.float32) * s, 'bq': jax.random.normal(ks[9], (E,), jnp.float32) * s, 'Wo': jax.random.normal(ks[10], (E, E), jnp.float32) * s, 'bo': jax.random.normal(ks[11], (E,), jnp.float32) * s}
        return inp
    _L3_xattn_all = _L3_xattn_setup()
    _L3_xattn_in = {k: v for k, v in _L3_xattn_all.items() if k in ('Wv', 'bv', 'Wk', 'bk', 'Wq', 'bq', 'Wo', 'bo')}
    del _L3_xattn_all

    def _L3_ffn_setup():
        import jax, jax.numpy as jnp
        import numpy as np
        IN_DIM = 128
        HIDDEN = 128
        OUT_DIM = 128
        NUM_EXPERTS = 16
        TOP_K = 2
        ROUTER_TEMP = 1.0
        LN_EPS = 1e-05

        def _layernorm(h, g, b):
            mu = jnp.mean(h, axis=-1, keepdims=True)
            var = jnp.mean(jnp.square(h - mu), axis=-1, keepdims=True)
            return (h - mu) * jax.lax.rsqrt(var + LN_EPS) * g + b
        key = jax.random.key(seed)
        ks = jax.random.split(key, 8)
        s_in = 1.0 / np.sqrt(IN_DIM)
        s_h = 1.0 / np.sqrt(HIDDEN)
        x = jax.random.normal(ks[0], (4, 256, IN_DIM), dtype=jnp.float32)
        Wr = jax.random.uniform(ks[1], (IN_DIM, NUM_EXPERTS), jnp.float32, -s_in, s_in)
        br = jax.random.uniform(ks[2], (NUM_EXPERTS,), jnp.float32, -s_in, s_in)
        W1 = jax.random.uniform(ks[3], (NUM_EXPERTS, IN_DIM, HIDDEN), jnp.float32, -s_in, s_in)
        b1 = jax.random.uniform(ks[4], (NUM_EXPERTS, HIDDEN), jnp.float32, -s_in, s_in)
        g1 = jnp.ones((NUM_EXPERTS, HIDDEN), jnp.float32)
        be1 = jnp.zeros((NUM_EXPERTS, HIDDEN), jnp.float32)
        W2 = jax.random.uniform(ks[5], (NUM_EXPERTS, HIDDEN, OUT_DIM), jnp.float32, -s_h, s_h)
        b2 = jax.random.uniform(ks[6], (NUM_EXPERTS, OUT_DIM), jnp.float32, -s_h, s_h)
        return {'x': x, 'Wr': Wr, 'br': br, 'W1': W1, 'b1': b1, 'g1': g1, 'be1': be1, 'W2': W2, 'b2': b2}
    _L3_ffn_all = _L3_ffn_setup()
    _L3_ffn_in = {k: v for k, v in _L3_ffn_all.items() if k in ('Wr', 'br', 'W1', 'b1', 'g1', 'be1', 'W2', 'b2')}
    del _L3_ffn_all
    return {'x': x, 'ctx_1024': ctx_1024, 'mask_Bx1xSxS2_if1': mask_Bx1xSxS2_if1, 'mask_BxS2_ik0': mask_BxS2_ik0, 'mask_Bx1xSxS2_ik1': mask_Bx1xSxS2_ik1, 'g_xattn': g_xattn, 'g_ffn': g_ffn, 'L0_xattn_Wq': _L0_xattn_in['Wq'], 'L0_xattn_Wk': _L0_xattn_in['Wk'], 'L0_xattn_Wv': _L0_xattn_in['Wv'], 'L0_xattn_Wo': _L0_xattn_in['Wo'], 'L0_xattn_bo': _L0_xattn_in['bo'], 'L0_ffn_expert_embeddings': _L0_ffn_in['expert_embeddings'], 'L0_ffn_first_linear': _L0_ffn_in['first_linear'], 'L0_ffn_second_linear': _L0_ffn_in['second_linear'], 'L1_xattn_Wq': _L1_xattn_in['Wq'], 'L1_xattn_Wk': _L1_xattn_in['Wk'], 'L1_xattn_Wv': _L1_xattn_in['Wv'], 'L1_xattn_Wo': _L1_xattn_in['Wo'], 'L1_ffn_gate_w': _L1_ffn_in['gate_w'], 'L1_ffn_gate_b': _L1_ffn_in['gate_b'], 'L1_ffn_shared_wg': _L1_ffn_in['shared_wg'], 'L1_ffn_shared_wu': _L1_ffn_in['shared_wu'], 'L1_ffn_shared_wd': _L1_ffn_in['shared_wd'], 'L1_ffn_experts_wg': _L1_ffn_in['experts_wg'], 'L1_ffn_experts_wu': _L1_ffn_in['experts_wu'], 'L1_ffn_experts_wd': _L1_ffn_in['experts_wd'], 'L2_xattn_Wq': _L2_xattn_in['Wq'], 'L2_xattn_bq': _L2_xattn_in['bq'], 'L2_xattn_Wk': _L2_xattn_in['Wk'], 'L2_xattn_bk': _L2_xattn_in['bk'], 'L2_xattn_Wv': _L2_xattn_in['Wv'], 'L2_xattn_bv': _L2_xattn_in['bv'], 'L2_xattn_Wo': _L2_xattn_in['Wo'], 'L2_xattn_bo': _L2_xattn_in['bo'], 'L2_ffn_gate_w': _L2_ffn_in['gate_w'], 'L2_ffn_gate_bias': _L2_ffn_in['gate_bias'], 'L2_ffn_w1': _L2_ffn_in['w1'], 'L2_ffn_w2': _L2_ffn_in['w2'], 'L2_ffn_w3': _L2_ffn_in['w3'], 'L2_ffn_sw1': _L2_ffn_in['sw1'], 'L2_ffn_sw2': _L2_ffn_in['sw2'], 'L2_ffn_sw3': _L2_ffn_in['sw3'], 'L3_xattn_Wv': _L3_xattn_in['Wv'], 'L3_xattn_bv': _L3_xattn_in['bv'], 'L3_xattn_Wk': _L3_xattn_in['Wk'], 'L3_xattn_bk': _L3_xattn_in['bk'], 'L3_xattn_Wq': _L3_xattn_in['Wq'], 'L3_xattn_bq': _L3_xattn_in['bq'], 'L3_xattn_Wo': _L3_xattn_in['Wo'], 'L3_xattn_bo': _L3_xattn_in['bo'], 'L3_ffn_Wr': _L3_ffn_in['Wr'], 'L3_ffn_br': _L3_ffn_in['br'], 'L3_ffn_W1': _L3_ffn_in['W1'], 'L3_ffn_b1': _L3_ffn_in['b1'], 'L3_ffn_g1': _L3_ffn_in['g1'], 'L3_ffn_be1': _L3_ffn_in['be1'], 'L3_ffn_W2': _L3_ffn_in['W2'], 'L3_ffn_b2': _L3_ffn_in['b2']}

def reference(x, ctx_1024, mask_Bx1xSxS2_if1, mask_BxS2_ik0, mask_Bx1xSxS2_ik1, g_xattn, g_ffn, L0_xattn_Wq, L0_xattn_Wk, L0_xattn_Wv, L0_xattn_Wo, L0_xattn_bo, L0_ffn_expert_embeddings, L0_ffn_first_linear, L0_ffn_second_linear, L1_xattn_Wq, L1_xattn_Wk, L1_xattn_Wv, L1_xattn_Wo, L1_ffn_gate_w, L1_ffn_gate_b, L1_ffn_shared_wg, L1_ffn_shared_wu, L1_ffn_shared_wd, L1_ffn_experts_wg, L1_ffn_experts_wu, L1_ffn_experts_wd, L2_xattn_Wq, L2_xattn_bq, L2_xattn_Wk, L2_xattn_bk, L2_xattn_Wv, L2_xattn_bv, L2_xattn_Wo, L2_xattn_bo, L2_ffn_gate_w, L2_ffn_gate_bias, L2_ffn_w1, L2_ffn_w2, L2_ffn_w3, L2_ffn_sw1, L2_ffn_sw2, L2_ffn_sw3, L3_xattn_Wv, L3_xattn_bv, L3_xattn_Wk, L3_xattn_bk, L3_xattn_Wq, L3_xattn_bq, L3_xattn_Wo, L3_xattn_bo, L3_ffn_Wr, L3_ffn_br, L3_ffn_W1, L3_ffn_b1, L3_ffn_g1, L3_ffn_be1, L3_ffn_W2, L3_ffn_b2):
    import jax
    import jax.numpy as jnp

    def _L0_xattn_ref(key, query, value, mask, Wq, Wk, Wv, Wo, bo):
        import jax, jax.numpy as jnp
        import numpy as np
        D_MODEL = 128
        HEADS = 16
        HEAD_DIM = D_MODEL // HEADS
        B, S = (2, 256)
        b, q_len, d = query.shape
        k_len = key.shape[1]
        h, hd = (HEADS, HEAD_DIM)
        q = (query @ Wq.T).reshape(b, q_len, h, hd)
        k = (key @ Wk.T).reshape(b, k_len, h, hd)
        v = (value @ Wv.T).reshape(b, k_len, h, hd)
        product = jnp.einsum('bqhd,bkhd->bhqk', q, k)
        product = jnp.where(mask == 0, jnp.float32(-1e+20), product)
        product = product / jnp.sqrt(jnp.asarray(hd, product.dtype))
        scores = jax.nn.softmax(product, axis=-1)
        out = jnp.einsum('bhqk,bkhd->bqhd', scores, v).reshape(b, q_len, h * hd)
        return out @ Wo.T + bo

    def _L0_ffn_ref(x, expert_embeddings, first_linear, second_linear):
        import jax, jax.numpy as jnp
        import numpy as np
        import math
        B, S, H = (8, 512, 128)
        E, I, K = (8, 256, 2)
        CAP_FACTOR = 1.0

        def _router(x, expert_embeddings):
            dot = jnp.einsum('bsh,eh->bse', x, expert_embeddings)
            n = dot.shape[0] * dot.shape[1]
            dot2 = dot.reshape(n, E)
            vals, idx = jax.lax.top_k(dot2, K)
            rows = jnp.arange(n)[:, None]
            masked = jnp.full_like(dot2, -jnp.inf).at[rows, idx].set(vals)
            return jax.nn.softmax(masked, axis=-1)
        batch, seq, hidden = x.shape
        n_tokens = batch * seq
        expert_capacity = math.ceil(n_tokens / E * CAP_FACTOR)
        weights = _router(x, expert_embeddings)
        ones = (weights > 0).astype(weights.dtype)
        cap_ones = jnp.where(jnp.cumsum(ones, axis=0) <= expert_capacity, ones, 0.0)
        caw = weights * cap_ones
        vals, idx = jax.lax.top_k(caw.T, expert_capacity)
        index = idx.reshape(-1)
        x_flat = x.reshape(n_tokens, hidden)
        tokens = x_flat[index].reshape(E, expert_capacity, hidden)
        inter = jax.nn.relu(jnp.einsum('ech,eih->eci', tokens, first_linear))
        out = jnp.einsum('eci,ehi->ech', inter, second_linear)
        out = out * vals[:, :, None]
        final = jnp.zeros((n_tokens, hidden), x.dtype).at[index].add(out.reshape(-1, hidden))
        return final.reshape(x.shape)

    def _L1_xattn_ref(query, key, value, Wq, Wk, Wv, Wo):
        import jax, jax.numpy as jnp
        import numpy as np
        B, S, D, H = (2, 256, 128, 16)
        HD = D // H
        SCALE = HD ** (-0.5)
        NEG = -1000000000.0
        b, sq, d = query.shape
        sk = key.shape[1]
        q = (query @ Wq.T).reshape(b, sq, H, HD).transpose(0, 2, 1, 3)
        k = (key @ Wk.T).reshape(b, sk, H, HD).transpose(0, 2, 1, 3)
        v = (value @ Wv.T).reshape(b, sk, H, HD).transpose(0, 2, 1, 3)
        scores = jnp.einsum('bhqd,bhkd->bhqk', q, k) * SCALE
        causal = jnp.arange(sq)[:, None] >= jnp.arange(sk)[None, :]
        scores = jnp.where(causal[None, None], scores, NEG)
        attn = jax.nn.softmax(scores, axis=-1)
        out = jnp.einsum('bhqk,bhkd->bhqd', attn, v)
        out = out.transpose(0, 2, 1, 3).reshape(b, sq, d)
        return out @ Wo.T

    def _L1_ffn_ref(x, gate_w, gate_b, shared_wg, shared_wu, shared_wd, experts_wg, experts_wu, experts_wd):
        import jax, jax.numpy as jnp
        import numpy as np
        B, S, D = (2, 256, 128)
        I = 64
        E = 16
        TOP_K = 2

        def _mlp(x, wg, wu, wd):
            return jnp.einsum('bsi,id->bsd', jax.nn.silu(x @ wg) * (x @ wu), wd)
        router_logits = jax.nn.sigmoid(x @ gate_w + gate_b)
        expert_values, expert_indices = jax.lax.top_k(router_logits, k=TOP_K)
        expert_values = expert_values / jnp.sum(expert_values, axis=-1, keepdims=True)
        hg = jnp.einsum('bsd,edi->bsei', x, experts_wg)
        hu = jnp.einsum('bsd,edi->bsei', x, experts_wu)
        all_outputs = jnp.einsum('bsei,eid->bsed', jax.nn.silu(hg) * hu, experts_wd)
        selected = jnp.take_along_axis(all_outputs, expert_indices[..., None], axis=2)
        expert_weighted = jnp.sum(expert_values[..., None] * selected, axis=2)
        return x + _mlp(x, shared_wg, shared_wu, shared_wd) + expert_weighted

    def _L2_xattn_ref(query, key, value, mask, Wq, bq, Wk, bk, Wv, bv, Wo, bo):
        import jax, jax.numpy as jnp
        import numpy as np
        B, S, D, H = (2, 256, 128, 16)
        HD = D // H

        def _split_heads(x):
            Bb, Ss, Dd = x.shape
            return x.reshape(Bb, Ss, H, HD).transpose(0, 2, 1, 3)
        q = _split_heads(query @ Wq.T + bq)
        k = _split_heads(key @ Wk.T + bk)
        v = _split_heads(value @ Wv.T + bv)
        scores = jnp.einsum('bhqd,bhkd->bhqk', q, k) / np.sqrt(HD).astype(np.float32)
        scores = jnp.where(mask[:, None, None, :] == 0, jnp.float32(-1000000000.0), scores)
        attn = jax.nn.softmax(scores, axis=-1)
        x = jnp.einsum('bhqk,bhkd->bhqd', attn, v)
        x = x.transpose(0, 2, 1, 3).reshape(query.shape[0], query.shape[1], D)
        return x @ Wo.T + bo

    def _L2_ffn_ref(x, gate_w, gate_bias, w1, w2, w3, sw1, sw2, sw3):
        import jax, jax.numpy as jnp
        import numpy as np
        DIM = 128
        INTER = 256
        E = 8
        TOPK = 2
        ROUTE_SCALE = 1.0

        def _mlp(x, w1, w2, w3):
            h = jax.nn.silu(x @ w1.T) * (x @ w3.T)
            return h @ w2.T
        shape = x.shape
        xt = x.reshape(-1, DIM)
        T = xt.shape[0]
        logits = xt @ gate_w.T
        scores = jax.nn.softmax(logits.astype(jnp.float32), axis=-1)
        original_scores = scores
        biased = scores + gate_bias
        _, indices = jax.lax.top_k(biased, TOPK)
        weights = jnp.take_along_axis(original_scores, indices, axis=1)
        weights = (weights * ROUTE_SCALE).astype(x.dtype)
        combine = (jax.nn.one_hot(indices, E, dtype=weights.dtype) * weights[..., None]).sum(axis=1)
        y = jnp.zeros_like(xt)
        for e in range(E):
            y = y + _mlp(xt, w1[e], w2[e], w3[e]) * combine[:, e:e + 1]
        z = _mlp(xt, sw1, sw2, sw3)
        return (y + z).reshape(shape)

    def _L3_xattn_ref(value, key, query, mask, Wv, bv, Wk, bk, Wq, bq, Wo, bo):
        import jax, jax.numpy as jnp
        import numpy as np
        N, S, E, H = (4, 256, 128, 16)
        D = E // H
        n, q_len = (query.shape[0], query.shape[1])
        v = (value @ Wv.T + bv).reshape(n, -1, H, D)
        k = (key @ Wk.T + bk).reshape(n, -1, H, D)
        q = (query @ Wq.T + bq).reshape(n, -1, H, D)
        qk = jnp.einsum('nqhd,nkhd->nhqk', q, k)
        qk = jnp.where(mask == 0, jnp.asarray(1e-20, qk.dtype), qk)
        attn = jax.nn.softmax(qk / jnp.asarray(np.sqrt(E), qk.dtype), axis=3)
        out = jnp.einsum('nhqk,nkhd->nqhd', attn, v).reshape(n, q_len, H * D)
        return out @ Wo.T + bo

    def _L3_ffn_ref(x, Wr, br, W1, b1, g1, be1, W2, b2):
        import jax, jax.numpy as jnp
        import numpy as np
        IN_DIM = 128
        HIDDEN = 128
        OUT_DIM = 128
        NUM_EXPERTS = 16
        TOP_K = 2
        ROUTER_TEMP = 1.0
        LN_EPS = 1e-05

        def _layernorm(h, g, b):
            mu = jnp.mean(h, axis=-1, keepdims=True)
            var = jnp.mean(jnp.square(h - mu), axis=-1, keepdims=True)
            return (h - mu) * jax.lax.rsqrt(var + LN_EPS) * g + b
        orig_shape = x.shape[:-1]
        x_flat = x.reshape(-1, x.shape[-1])
        logits = (x_flat @ Wr + br) / max(ROUTER_TEMP, 1e-06)
        probs = jax.nn.softmax(logits, axis=-1)
        topk_w, topk_idx = jax.lax.top_k(probs, TOP_K)
        topk_w = topk_w / jnp.clip(jnp.sum(topk_w, axis=-1, keepdims=True), 1e-09)
        h = jnp.einsum('nc,ech->neh', x_flat, W1) + b1
        h = _layernorm(h, g1, be1)
        h = jax.nn.gelu(h, approximate=False)
        expert_out = jnp.einsum('neh,eho->neo', h, W2) + b2
        sel = jnp.take_along_axis(expert_out, topk_idx[:, :, None], axis=1)
        y_flat = jnp.sum(sel * topk_w[:, :, None], axis=1)
        return y_flat.reshape(*orig_shape, y_flat.shape[-1])
    x = x + jnp.tanh(g_xattn[0]) * _L0_xattn_ref(ctx_1024, _layernorm(x, axis=-1), ctx_1024, mask_Bx1xSxS2_if1, L0_xattn_Wq, L0_xattn_Wk, L0_xattn_Wv, L0_xattn_Wo, L0_xattn_bo)
    x = x + jnp.tanh(g_ffn[0]) * _L0_ffn_ref(_layernorm(x, axis=-1), L0_ffn_expert_embeddings, L0_ffn_first_linear, L0_ffn_second_linear)
    x = x + jnp.tanh(g_xattn[1]) * _L1_xattn_ref(_layernorm(x, axis=-1), ctx_1024, ctx_1024, L1_xattn_Wq, L1_xattn_Wk, L1_xattn_Wv, L1_xattn_Wo)
    x = x + jnp.tanh(g_ffn[1]) * _L1_ffn_ref(_layernorm(x, axis=-1), L1_ffn_gate_w, L1_ffn_gate_b, L1_ffn_shared_wg, L1_ffn_shared_wu, L1_ffn_shared_wd, L1_ffn_experts_wg, L1_ffn_experts_wu, L1_ffn_experts_wd)
    x = x + jnp.tanh(g_xattn[2]) * _L2_xattn_ref(_layernorm(x, axis=-1), ctx_1024, ctx_1024, mask_BxS2_ik0, L2_xattn_Wq, L2_xattn_bq, L2_xattn_Wk, L2_xattn_bk, L2_xattn_Wv, L2_xattn_bv, L2_xattn_Wo, L2_xattn_bo)
    x = x + jnp.tanh(g_ffn[2]) * _L2_ffn_ref(_layernorm(x, axis=-1), L2_ffn_gate_w, L2_ffn_gate_bias, L2_ffn_w1, L2_ffn_w2, L2_ffn_w3, L2_ffn_sw1, L2_ffn_sw2, L2_ffn_sw3)
    x = x + jnp.tanh(g_xattn[3]) * _L3_xattn_ref(ctx_1024, ctx_1024, _layernorm(x, axis=-1), mask_Bx1xSxS2_ik1, L3_xattn_Wv, L3_xattn_bv, L3_xattn_Wk, L3_xattn_bk, L3_xattn_Wq, L3_xattn_bq, L3_xattn_Wo, L3_xattn_bo)
    x = x + jnp.tanh(g_ffn[3]) * _L3_ffn_ref(_layernorm(x, axis=-1), L3_ffn_Wr, L3_ffn_br, L3_ffn_W1, L3_ffn_b1, L3_ffn_g1, L3_ffn_be1, L3_ffn_W2, L3_ffn_b2)
    return x

_drawn_inputs = setup_inputs


def setup_inputs(seed=0):
    import zlib

    import numpy as np

    out = dict(_drawn_inputs(seed))
    spreads = {'L1_ffn_gate_b': (0.0, 0.1),
     'L2_xattn_bq': (0.0, 0.585),
     'L2_xattn_bk': (0.0, 2.0),
     'L2_xattn_bv': (0.0, 0.1),
     'L2_xattn_bo': (0.0, 0.1),
     'L3_ffn_g1': (1.0, 0.6),
     'L3_ffn_be1': (0.0, 0.784)}
    factors = {'L0_xattn_Wq': 6.13,
     'L0_xattn_Wk': 8.0,
     'L2_ffn_gate_w': 8.0,
     'L2_ffn_gate_bias': 8.0,
     'L2_ffn_w1': 8.0,
     'L2_ffn_w2': 8.0,
     'L2_ffn_w3': 8.0,
     'L2_ffn_sw1': 8.0,
     'L2_ffn_sw2': 8.0,
     'L2_ffn_sw3': 8.0,
     'L3_xattn_Wk': 2.889,
     'L3_xattn_bk': 64.0,
     'L3_xattn_Wq': 2.835,
     'L3_xattn_bq': 8.0,
     'L3_ffn_b1': 5.832,
     'L3_ffn_b2': 4.098,
     'L3_xattn_bv': 3.0,
     'L3_xattn_bo': 3.444}
    for name, (base, spread) in spreads.items():
        noise = np.random.default_rng([zlib.crc32(name.encode()), seed]).standard_normal(out[name].shape)
        drawn = base * np.exp(spread * noise) if base else spread * noise
        out[name] = jnp.asarray(drawn.astype(out[name].dtype))
    for name, factor in factors.items():
        out[name] = (out[name] * factor).astype(out[name].dtype)
    return out
```

```python
from contextlib import ExitStack

import concourse.bass as bass
from concourse import mybir

F32, F16, BF16 = mybir.dt.float32, mybir.dt.float16, mybir.dt.bfloat16
I32, U32 = mybir.dt.int32, mybir.dt.uint32
ALU, ACT, AX = mybir.AluOpType, mybir.ActivationFunctionType, mybir.AxisListType

LAYERS, D, HEADS, HD, SEQ, BATCH = 4, 128, 16, 8, 64, 128
TOK = BATCH * SEQ
TILE = 128
NT = 4
BLK = NT * TILE
NB = TOK // BLK
EXPERTS = [8, 16, 8, 16]
CAPACITY = -(-TOK // EXPERTS[0])
EPS = 1e-5
MASKED = -1e20
WS = 64.0
SCORE_SCALE = [HD ** -0.5, HD ** -0.5, HD ** -0.5, D ** -0.5]
MOE_COLS = [4096, 3328, 6912, 4096]
MOE_BASE = [sum(MOE_COLS[:i]) for i in range(LAYERS)]
W_AT = [0, MOE_COLS[2], 0, MOE_COLS[2]]
W_COLS = MOE_COLS[2] + MOE_COLS[3]
PIECES = [4, 4, 6, 4]
UNITS = [16, 9, 18, 16]
ROUTE_STEPS = [20, 14, 17, 20]
HW_POOL = [0, 8, 16, 0]
LATE = [1, 1, 1, 2]


def ring_plan(layer):
    if layer == 0:
        uses = [True, False, False] * 8
    elif layer == 1:
        uses = [True, True, False] * 8 + [True, False]
    elif layer == 2:
        uses = ([True] + [True, False] * 2) * 8 + [True, False] * 2
    else:
        uses = [True] * 16 + [False, False] * 16
    return uses + [False]


RING = [ring_plan(layer) for layer in range(LAYERS)]
RING_ACT = [sum(r) for r in RING]
RING_DVE = [len(r) - sum(r) - 1 for r in RING]
RING_OF = [
    [[3 * (u // 2)] * (u % 2 == 0) + [3 * (u // 2) + 1 + u % 2] for u in range(16)],
    [[3 * u, 3 * u + 1, 3 * u + 2] if u < 8 else [24, 25] for u in range(9)],
    [([5 * (u // 2)] * (u % 2 == 0) + [5 * (u // 2) + 1 + 2 * (u % 2), 5 * (u // 2) + 2 + 2 * (u % 2)])
     if u < 16 else [40 + 2 * (u - 16), 41 + 2 * (u - 16)] for u in range(18)],
    [[15 + 2 * u if u else 16, min(18 + 2 * u, 47)] for u in range(16)],
]


def turn(mix, attend, prepare, split=None):
    steps = []
    if mix:
        layer, b = mix
        n = UNITS[layer] + LATE[layer] + 1
        names = [("m_start", 0)]
        if layer == 3:
            names += [("m_pre", e) for e in range(EXPERTS[3] + 2)] + [("m_mid", 0)]
        names += [("m_unit", u) for u in range(n)]
        for i, (name, k) in enumerate(names):
            steps.append((0.001 + 0.95 * i / len(names), name, layer, b, k))
        steps.append((0.985, "m_end", layer, b, 0))
    if attend:
        layer, b = attend
        for t in range(NT):
            steps.append((0.0 + 0.06 * t, "q_scores", layer, b, t))
            steps.append((0.24, "q_exp", layer, b, t))
            at = 0.30 + 0.115 * t
            steps.append((at, "q_turn_a", layer, b, t))
            steps.append((at + 0.025, "q_turn_b", layer, b, t))
            steps.append((at + 0.05, "q_pv", layer, b, t))
            steps.append((at + 0.085, "q_oturn", layer, b, t))
            steps.append((at + 0.11, "q_out", layer, b, t))
        steps.append((0.80, "f_norm", layer, b, 0))
        steps.append((0.84, "f_turn", layer, b, 0))
        steps.append((0.87, "f_route", layer, b, 0))
        steps.append((0.96, "f_wturn", layer, b, 0))
    if prepare:
        layer, b = prepare
        steps.append((0.26, "p_load", layer, b, 0))
        steps.append((0.31, "p_norm", layer, b, 0))
        steps.append((0.37, "p_turn", layer, b, 0))
        steps.append((0.41, "p_q", layer, b, 0))
        steps.append((0.45, "p_k", layer, b, 0))
        steps.append((0.79, "p_v", layer, b, 0))
    if split is not None:
        for i in range(PIECES[split]):
            steps.append((0.2 + 0.1 * i, "w_split", split, 0, i))
    steps.sort(key=lambda s: s[0])
    return [s[1:] for s in steps]


def walk(eng, steps, enter):

    def run(sequence):
        for name, layer, b, k in sequence:
            if name in steps:
                steps[name](layer, b, k)

    run([("w_split", 0, 0, i) for i in range(PIECES[0])])
    run(turn(None, None, (0, 0)))
    run(turn(None, (0, 0), (0, 1)))
    for layer in range(LAYERS):
        enter(layer)
        run(turn((layer, 0), (layer, 1), (layer, 2)))
        with eng.Fori(1, NB - 2) as i:
            run(turn((layer, i), (layer, i + 1), (layer, i + 2)))
        last = layer == LAYERS - 1
        run(turn((layer, NB - 2), (layer, NB - 1), None if last else (layer + 1, 0),
                 None if last else layer + 1))
        run(turn((layer, NB - 1), None if last else (layer + 1, 0), None if last else (layer + 1, 1)))


class Signal:

    def __init__(self, sem, per_block):
        self.sem = sem
        self.n = per_block if isinstance(per_block, list) else [per_block] * LAYERS
        self.base = [NB * sum(self.n[:i]) for i in range(LAYERS)]

    def count(self, layer, b, k):
        return b * self.n[layer] + (self.base[layer] + k)


def build(nc, x_in, ctx_in, m0_in, m2_in, m3_in, watt_in, wmoe_in, wrt_in, rows_in, cols_in, bc_in,
          b1_in, b2_in, cst_in, out):
    scratch_q = nc.dram_tensor("scratch_q", (4, 128, BLK), F16).ap()
    scratch_k = nc.dram_tensor("scratch_k", (4, 128, BLK), F16).ap()

    with ExitStack() as ctx:
        def sb(name, shape, dt=F32):
            return ctx.enter_context(nc.sbuf_tensor(name, shape, dt))

        def sem(name):
            return ctx.enter_context(nc.semaphore(name))

        def signal(name, per_block=1):
            return Signal(sem(name), per_block)

        xs = sb("xs", [128, NB * NT * D])
        w_hi = sb("w_hi", [128, W_COLS], F16)
        w_lo = sb("w_lo", [128, W_COLS], F16)
        w_att = sb("w_att", [128, LAYERS, 4, D])
        w_rt = sb("w_rt", [128, 48])
        rows = sb("rows", [1, 416])
        cols = sb("cols", [128, 40])
        bc = sb("bc", [128, LAYERS * D + 8 + 8])
        cst = sb("cst", [128, 360])
        b1 = sb("b1", [16, D])
        b2 = sb("b2", [48, D])
        gate = sb("gate", [128, 8])
        gate_ffn = sb("gate_ffn", [128, 4])
        ident_bf = sb("ident_bf", [128, 128], BF16)
        ident_ws = sb("ident_ws", [128, 128], F16)
        tri = sb("tri", [128, 128], BF16)
        ones_bf = sb("ones_bf", [128, 128], BF16)
        ones_row = sb("ones_row", [1, 128])
        mean_col = sb("mean_col", [128, 1])
        eps_col = sb("eps_col", [128, 1])
        neg_half = sb("neg_half", [128, NT])
        causal = sb("causal", [128, SEQ], BF16)
        sel8 = sb("sel8", [24, 8], BF16)
        sel16 = sb("sel16", [48, 16], BF16)
        b1_col = sb("b1_col", [128, 16])
        b1_mean = sb("b1_mean", [16, 1])
        b2_part = sb("b2_part", [48, 3, D], BF16)
        w_mean = sb("w_mean", [128, 16])
        hidden = sb("hidden", [128, 16, BLK])
        staging = hidden[:, :, :].rearrange("p e n -> p (e n)")
        ctxT = sb("ctxT", [128, BLK])
        m_raw = sb("m_raw", [128, NT, SEQ], I32)
        m_add = sb("m_add", [128, NT, SEQ], BF16)
        m_mul = sb("m_mul", [128, NT, SEQ])
        p_st = sb("p_st", [128, NT, 6])
        p_mv = sb("p_mv", [128, NT, 2])
        p_ve = sb("p_ve", [128, NT])
        p_rs = sb("p_rs", [128, NT])
        xn_a = sb("xn_a", [128, NT, D])
        xnT_a = sb("xnT_a", [128, BLK])
        q_hl = sb("q_hl", [128, 2, BLK], F16)
        k_hl = sb("k_hl", [128, 2, BLK], F16)
        q_stack = sb("q_stack", [128, 4, BLK], F16)
        k_diag = sb("k_diag", [128, 4, 4, BLK], F16)
        v_diag = sb("v_diag", [128, NT, 8, 2, 2, HD + 1])
        prob = sb("prob", [128, NT, HEADS * SEQ])
        q_mx = sb("q_mx", [128, 2, 8])
        probT = sb("probT", [128, 2, 8, TILE])
        q_rc = sb("q_rc", [128, 8, 2])
        att = sb("att", [128, D])
        attT = sb("attT", [128, TILE])
        f_st = sb("f_st", [128, NT, 6])
        f_mv = sb("f_mv", [128, NT, 2])
        f_ve = sb("f_ve", [128, NT])
        f_rs = sb("f_rs", [128, NT])
        xn_f = sb("xn_f", [128, NT, D])
        xnT_f = sb("xnT_f", [128, BLK])
        r_lg = sb("r_lg", [128, NT, 16])
        r_ex = sb("r_ex", [128, NT, 16])
        r_val = sb("r_val", [128, NT, 16])
        r_key = sb("r_key", [128, NT, 16])
        r_oh = sb("r_oh", [128, 2, NT, 16])
        r_w = sb("r_w", [128, NT, 16])
        r_w2 = sb("r_w2", [128, NT, 16])
        r_rest = sb("r_rest", [128, 2, NT, 16])
        r_top = sb("r_top", [128, NT, 8])
        r_idx = sb("r_idx", [128, NT, 8], U32)
        r_idf = sb("r_idf", [128, NT, 8])
        r_s = sb("r_s", [128, 4, NT])
        r_one = sb("r_one", [128, NT, 8], BF16)
        r_sum = sb("r_sum", [128, 8])
        carry = sb("carry", [128, 8], BF16)
        w3 = sb("w3", [128, NT, 48], BF16)
        wT_next = sb("wT_next", [48, BLK], BF16)
        wT = sb("wT", [48, BLK], BF16)
        x_hi = sb("x_hi", [128, BLK], F16)
        x_lo = sb("x_lo", [128, BLK], F16)
        w_bc = sb("w_bc", [128, 2, BLK])
        act = sb("act", [128, 2, BLK])
        had = sb("had", [128, 2, BLK])
        hw = sb("hw", [128, 2, BLK])
        h_hi = sb("h_hi", [128, 2, BLK], F16)
        h_lo = sb("h_lo", [128, 2, BLK], F16)
        yT = sb("yT", [128, BLK])
        b2_rest = yT[0:48, 0:2 * D].rearrange("p (k d) -> p k d", k=2)
        sd = sb("sd", [128, NT, 16])
        rs = sb("rs", [128, NT, 16])
        rs_rest = sb("rs_rest", [128, 2, NT, 16])
        rs3 = sb("rs3", [128, NT, 48], BF16)
        rsT = sb("rsT", [48, BLK], BF16)

        ps = [ctx.enter_context(nc.psum_tensor(f"ps{i}", [128, 512], F32)) for i in range(8)]
        S, A, T, R, Y = ps[0:2], ps[2], ps[3], ps[4:7], ps[7]

        in_x = [sem("x_loaded_0"), sem("x_loaded_1"), sem("x_loaded_rest")]
        in_c = sem("constants_loaded")
        in_w = sem("expert_weights_loaded")
        w_hi_ok, w_lo_ok, w_cen = sem("w_hi_ready"), sem("w_lo_ready"), sem("w_centred")
        c_dve, c_pool, c_act, c_pe = sem("consts_dve"), sem("consts_pool"), sem("consts_act"), sem("consts_pe")
        stored = sem("out_stored")
        ctx_ok = signal("ctx_loaded", 16)
        mask_in = signal("mask_loaded", [16, 0, 32, 16])
        mask_ok = signal("mask_ready", [1, 0, 1, 1])
        p_stat, p_mom, p_var, p_rstd = signal("p_stats"), signal("p_moments"), signal("p_var_eps"), signal("p_rstd")
        p_xn, p_xT, p_xTs = signal("p_normed"), signal("p_turned"), signal("p_xT_saved")
        p_qp, p_kp = signal("q_projected"), signal("k_projected")
        p_qh, p_ql, p_kh, p_kl = signal("q_hi"), signal("q_lo"), signal("k_hi"), signal("k_lo")
        q_scr, k_scr, q_ok, k_ok = signal("q_in_dram", 64), signal("k_in_dram", 64), signal("q_stacked", 16), signal("k_stacked", 64)
        p_vp, p_vd = signal("v_projected", 2), signal("v_placed")
        s_ok = signal("scores_ready", 8)
        s_mul = signal("scores_masked", [0, 0, 0, 8])
        s_max, s_sub = signal("scores_max", 8), signal("scores_shifted", 8)
        e_ok = signal("exp_ready", 4)
        pt_ok, pt_a, pt_b = signal("probs_turned", 8), signal("probT_a_saved", 4), signal("probT_b_saved", 4)
        pv_ok, rc_ok, o_ok = signal("pv_ready", 4), signal("sums_inverted", 4), signal("att_ready", 4)
        ot_ok, ot_sv, out_ok, x_att = signal("att_turned", 4), signal("attT_saved", 4), signal("att_projected", 4), signal("x_attended", 4)
        f_stat, f_mom, f_var, f_rstd = signal("f_stats"), signal("f_moments"), signal("f_var_eps"), signal("f_rstd")
        f_xn, f_xT, f_xTs, f_lg = signal("f_normed"), signal("f_turned"), signal("f_xT_saved"), signal("logits_ready")
        rt = signal("route_step", ROUTE_STEPS)
        rt_act = signal("route_act", 1)
        cum_ok = signal("cumsum_ready", [1, 0, 0, 0])
        w3_ok, wt_ok, wt_sv = signal("weights_split"), signal("weights_turned"), signal("wT_saved")
        m_xh, m_xl, m_wc = signal("x_hi_ready"), signal("x_lo_ready"), signal("wT_copied")
        filled = signal("ring_filled", [len(r) for r in RING])
        read_act, read_dve = signal("ring_read_act", RING_ACT), signal("ring_read_dve", RING_DVE)
        hw_pool = signal("hidden_weighted", HW_POOL)
        hi_ok = signal("hidden_hi", UNITS)
        lo_ok = signal("hidden_lo", UNITS)
        y_ok = signal("unit_added", UNITS)
        gelu_ok = signal("gelu_ready", [0, 0, 0, 16])
        sq_ok, var_ok = signal("squares_ready", [0, 0, 0, 16]), signal("variances_ready", [0, 0, 0, 16])
        sd_ok, rs_ok, rs_tn, rs_sv = signal("sd_ready", [0, 0, 0, 1]), signal("rstd_split", [0, 0, 0, 6]), signal("rstd_turned", [0, 0, 0, 1]), signal("rsT_saved", [0, 0, 0, 1])
        yT_ok, x_mix = signal("yT_saved"), signal("x_mixed")

        def wait(eng, sig, layer, b, k, apart=False):
            value = sig.count(layer, b, k)
            if not (isinstance(value, int) and value <= 0):
                if apart and not isinstance(value, int):
                    value = eng.to_reg(value)
                    eng.wait_ge(c_dve, 1)
                eng.wait_ge(sig.sem, value)

        def tile_x(b, t, n=1):
            return xs[:, bass.ds((b * NT + t) * D, n * D)]

        def cast_row(ap, n):
            return ap.unsqueeze(2).to_broadcast([ap.shape[0], ap.shape[1], n])

        def wcol(hi, layer, at, n, rows_=128):
            w = w_hi if hi else w_lo
            return w[0:rows_, W_AT[layer] + at:W_AT[layer] + at + n]

        def w_free(eng, layer):
            if layer >= 2:
                wait(eng, y_ok, layer - 1, 0, 0)

        def ring_free(eng, layer, b, k, apart=False):
            if k == 0:
                wait(eng, x_mix, layer, b, 0, apart)
            elif k >= 3:
                by_act = RING[layer][k - 3]
                nth = sum(1 for r in RING[layer][:k - 2] if r == by_act)
                wait(eng, read_act if by_act else read_dve, layer, b, nth, apart)

        def act_read(layer, k):
            return sum(RING[layer][:k + 1])

        def dve_read(layer, k):
            return k + 1 - sum(RING[layer][:k + 1])

        def weighted(eng, layer, b, u):
            if u < HW_POOL[layer]:
                wait(eng, hw_pool, layer, b, u + 1)
            else:
                wait(eng, read_dve, layer, b, dve_read(layer, RING_OF[layer][u][-1]))

        def hi_free(eng, layer, b, u):
            wait(eng, y_ok, layer, b, max(u - 1, 0))

        def lo_part(eng, layer, b, u):
            m = 64 if layer == 1 and u == 8 else 128
            weighted(eng, layer, b, u)
            wait(eng, hi_ok, layer, b, u + 1)
            wait(eng, y_ok, layer, b, max(u - 1, 0))
            eng.tensor_tensor(h_lo[0:m, u % 2, :], hw[0:m, u % 2, :], h_hi[0:m, u % 2, :], ALU.subtract)\
               .then_inc(lo_ok.sem, 1)

        block = ctx.enter_context(nc.Block())

        @block.sync
        def _(sp):
            def load_x(n, b0, b1_):
                sp.dma_start(xs[:, b0 * NT * D:b1_ * NT * D].rearrange("p (t d) -> p t d", d=D),
                             x_in[b0 * BLK:b1_ * BLK, :].rearrange("(t p) d -> p t d", p=128)).then_inc(in_x[n], 16)

            load_x(0, 0, 1)
            sp.dma_start(cst[:, :], cst_in).then_inc(in_c, 16)
            sp.dma_start(w_att[:, :, :, :].rearrange("p a b c -> p (a b c)"), watt_in).then_inc(in_c, 16)
            sp.dma_start(cols[:, :], cols_in).then_inc(in_c, 16)
            sp.dma_start(bc[:, :], bc_in[0, :].partition_broadcast(128)).then_inc(in_c, 16)
            sp.dma_start(rows[:, :], rows_in).then_inc(in_c, 16)
            sp.dma_start(w_rt[:, :], wrt_in).then_inc(in_c, 16)
            sp.dma_start(b1[:, :], b1_in).then_inc(in_c, 16)
            sp.dma_start(b2[:, :], b2_in).then_inc(in_c, 16)
            load_x(1, 1, 2)

            def w_split(layer, b, k):
                if k == 0:
                    if layer:
                        sp.wait_ge(w_lo_ok, sum(PIECES[:layer]))
                        sp.wait_ge(w_hi_ok, sum(PIECES[:layer]))
                    sp.dma_start(staging[:, 0:MOE_COLS[layer]],
                                 wmoe_in[:, MOE_BASE[layer]:MOE_BASE[layer] + MOE_COLS[layer]]).then_inc(in_w, 16)

            def p_load(layer, b, k):
                wait(sp, p_vp, layer, b, 0, apart=True)
                wait(sp, p_kp, layer, b, 0, apart=True)
                sp.dma_start(ctxT[:, :], ctx_in[:, bass.ds(b * BLK, BLK)]).then_inc(ctx_ok.sem, 16)
                if layer == 1:
                    return
                wait(sp, mask_ok, layer, b, 0, apart=True)
                if layer == 2:
                    for half in range(2):
                        sp.dma_start(m_raw[64 * half:64 * half + 64, :, :].rearrange("p (o t) k -> p o (t k)", o=1),
                                     m2_in[bass.ds(b, 1), half, :].partition_broadcast(64))\
                            .then_inc(mask_in.sem, 16)
                else:
                    src = m0_in if layer == 0 else m3_in
                    sp.dma_start(m_raw[:, :, :], src[bass.ds(b * BLK, BLK), :].rearrange("(t p) k -> p t k", p=128))\
                        .then_inc(mask_in.sem, 16)

            def stack(layer, b, src, lo_signal, parts, scratch, in_dram):
                wait(sp, lo_signal, layer, b, 1, apart=True)
                to = scratch.rearrange("g (j t p) n -> t (g j) p n", j=4, t=4)
                for t in range(4):
                    sp.dma_start(to[t], src[:, parts[t], :]).then_inc(in_dram.sem, 16)
                wait(sp, in_dram, layer, b, 64, apart=True)

            def p_q(layer, b, k):
                stack(layer, b, q_hl, p_ql, (0, 0, 1, 1), scratch_q, q_scr)
                wait(sp, s_ok, layer, b, 0, apart=True)
                sp.dma_start(q_stack[:, :, :], scratch_q.rearrange("g p n -> p g n")).then_inc(q_ok.sem, 16)
                wait(sp, q_ok, layer, b, 16, apart=True)

            def p_k(layer, b, k):
                stack(layer, b, k_hl, p_kl, (0, 1, 0, 1), scratch_k, k_scr)
                wait(sp, s_ok, layer, b, 0, apart=True)
                if layer == 0 and isinstance(b, int) and b == 0:
                    sp.wait_ge(c_pool, 1)
                for j in range(4):
                    sp.dma_start(k_diag[32 * j:32 * j + 32, j, :, :],
                                 scratch_k[:, 32 * j:32 * j + 32, :].rearrange("g p n -> p g n")).then_inc(k_ok.sem, 16)
                wait(sp, k_ok, layer, b, 64, apart=True)

            def m_end(layer, b, k):
                if layer == LAYERS - 1:
                    wait(sp, x_mix, layer, b, 1, apart=True)
                    sp.dma_start(out[bass.ds(b * BLK, BLK), :].rearrange("(t p) d -> p t d", p=128),
                                 tile_x(b, 0, NT).rearrange("p (t d) -> p t d", d=D)).then_inc(stored, 16)

            def enter(layer):
                if layer == 0:
                    load_x(2, 2, NB)

            walk(sp, dict(w_split=w_split, p_load=p_load, p_q=p_q, p_k=p_k, m_end=m_end), enter)
            sp.wait_ge(stored, 16 * NB)

        @block.tensor
        def _(pe):
            mm = nc.tensor.matmul
            ident = cst[:, 0:128]
            pe.wait_ge(in_c, 128)
            pe.wait_ge(c_dve, 5)
            mm(A[:, 0:16], b1[:, :], ident[0:16, 0:16], is_transpose=True, start=True, stop=True).then_inc(c_pe, 1)
            pe.wait_ge(c_dve, 6)

            def enter(layer):
                pe.wait_ge(w_hi_ok, sum(PIECES[:layer + 1]))
                pe.wait_ge(w_lo_ok, sum(PIECES[:layer + 1]))

            def p_turn(layer, b, k):
                wait(pe, p_xn, layer, b, 1)
                wait(pe, s_sub, layer, b, 0)
                for t in range(NT):
                    last = mm(S[0][:, t * 128:t * 128 + 128], xn_a[:, t, :], ident, is_transpose=True, start=True, stop=True)
                last.then_inc(p_xT.sem, 1)

            def p_q(layer, b, k):
                wait(pe, ctx_ok, layer, b, 16)
                wait(pe, p_xTs, layer, b, 1)
                mm(S[1][:, :], w_att[:, layer, 0, :], xnT_a[:, :],
                   start=True, stop=True).then_inc(p_qp.sem, 1)

            def p_k(layer, b, k):
                mm(S[0][:, :], w_att[:, layer, 1, :], ctxT[:, :],
                   start=True, stop=True).then_inc(p_kp.sem, 1)

            def p_v(layer, b, k):
                for half, free in ((0, p_kl), (1, p_ql)):
                    wait(pe, free, layer, b, 1)
                    for i in range(4):
                        tb = 4 * half + i
                        for copy in range(2):
                            last = mm(S[half][64 * copy:64 * copy + 64, i * 128:i * 128 + 128],
                                      ctxT[:, 64 * tb:64 * tb + 64], w_att[:, layer, 2, :], start=True, stop=True)
                    last.then_inc(p_vp.sem, 1)

            def q_scores(layer, b, t):
                if t == 0:
                    wait(pe, q_ok, layer, b, 16)
                    wait(pe, k_ok, layer, b, 64)
                    wait(pe, p_vd, layer, b, 1)
                    if layer != 1:
                        wait(pe, mask_ok, layer, b, 1)
                for half in range(2):
                    if t:
                        wait(pe, s_sub, layer, b, 2 * t - 1 + half)
                    if layer != 3:
                        m = causal[:, :] if layer == 1 else m_add[:, t, :]
                        mm(S[half][:, :].rearrange("p (h k) -> p h k", h=8), ident_bf[:, :],
                           m.unsqueeze(1).to_broadcast([128, 8, SEQ]), start=True, stop=False, skip_group_check=True)
                    for g in (2 * half, 2 * half + 1):
                        for e in range(2):
                            at = t * TILE + e * SEQ
                            last = mm(S[half][64 * e:64 * e + 64, (g % 2) * 256:(g % 2) * 256 + 256].rearrange("p (j k) -> p j k", j=4),
                                      q_stack[:, g, at:at + SEQ], k_diag[:, :, g, at:at + SEQ],
                                      start=(layer == 3), stop=True, skip_group_check=True)
                    last.then_inc(s_ok.sem, 1)

            def q_turn(layer, b, t, half):
                if half == 0:
                    wait(pe, e_ok, layer, b, t + 1)
                    if t == 0:
                        wait(pe, wt_sv, layer, b, 0)
                    else:
                        wait(pe, ot_sv, layer, b, t)
                else:
                    wait(pe, pt_a, layer, b, t + 1)
                for i in range(4):
                    j = 4 * half + i
                    last = mm(T[:, i * 128:i * 128 + 128], prob[:, t, j * 128:j * 128 + 128], ident,
                              is_transpose=True, start=True, stop=True)
                last.then_inc(pt_ok.sem, 1)

            def q_pv(layer, b, t):
                wait(pe, pt_a, layer, b, t + 1)
                wait(pe, pt_b, layer, b, t + 1)
                if t == 0:
                    wait(pe, f_xTs, layer, b, 0)
                    wait(pe, rt, layer, b, 0)
                else:
                    wait(pe, x_att, layer, b, t)
                for j in range(8):
                    last = mm(A[:, 36 * j:36 * j + 36], probT[:, t % 2, j, :],
                              v_diag[:, t, j, :, :, :].rearrange("p b h d -> p (b h d)"), start=True, stop=True)
                last.then_inc(pv_ok.sem, 1)

            def q_oturn(layer, b, t):
                wait(pe, o_ok, layer, b, t + 1)
                wait(pe, pt_b, layer, b, t + 1)
                mm(T[:, 0:128], att[:, :], ident, is_transpose=True, start=True, stop=True).then_inc(ot_ok.sem, 1)

            def q_out(layer, b, t):
                wait(pe, ot_sv, layer, b, t + 1)
                row = {0: 0, 2: 128, 3: 256}.get(layer)
                last = mm(A[:, 0:128], attT[:, :], w_att[:, layer, 3, :], start=True, stop=row is None)
                if row is not None:
                    last = mm(A[:, 0:128], ones_row[:, :], rows[:, row:row + 128], start=False, stop=True)
                last.then_inc(out_ok.sem, 1)

            def f_turn(layer, b, k):
                wait(pe, f_xn, layer, b, 1)
                wait(pe, x_att, layer, b, 4)
                for t in range(NT):
                    last = mm(A[:, t * 128:t * 128 + 128], xn_f[:, t, :], ident, is_transpose=True, start=True, stop=True)
                last.then_inc(f_xT.sem, 1)

            def f_route(layer, b, k):
                E = EXPERTS[layer]
                at = (0, 8, 24, 32)[layer]
                row = {1: 384, 3: 400}.get(layer)
                wait(pe, f_xTs, layer, b, 1)
                wait(pe, ot_sv, layer, b, 4)
                for t in range(NT):
                    last = mm(T[:, t * E:t * E + E], xnT_f[:, t * 128:t * 128 + 128], w_rt[:, at:at + E],
                              start=True, stop=row is None)
                    if row is not None:
                        last = mm(T[:, t * E:t * E + E], ones_row[:, :], rows[:, row:row + E], start=False, stop=True)
                last.then_inc(f_lg.sem, 1)
                if layer == 0:
                    wait(pe, rt, 0, b, 13)
                    for t in range(NT):
                        o = A[:, 8 * t:8 * t + 8]
                        mm(o, tri[:, :], r_one[:, t, :], start=True, stop=False)
                        for s in range(t):
                            mm(o, ones_bf[:, :], r_one[:, s, :], start=False, stop=False)
                        last = mm(o, ones_bf[:, :], carry[:, :], start=False, stop=True)
                    last.then_inc(cum_ok.sem, 1)

            def f_wturn(layer, b, k):
                n = 3 * EXPERTS[layer]
                wait(pe, w3_ok, layer, b, 1, apart=True)
                to = T[0:n, :].bitcast(BF16)
                for t in range(NT):
                    last = mm(to[:, t * 128:t * 128 + 128], w3[:, t, 0:n], ident_bf[:, :], is_transpose=True, start=True, stop=True)
                last.then_inc(wt_ok.sem, 1)

            def m_start(layer, b, k):
                wait(pe, m_xl, layer, b, 1)
                wait(pe, m_wc, layer, b, 1)

            def fill(layer, b, k, pairs, m=128):
                ring_free(pe, layer, b, k)
                for n, (lhs, rhs) in enumerate(pairs):
                    last = mm(R[k % 3][0:m, :], lhs, rhs, start=(n == 0), stop=(n == len(pairs) - 1))
                last.then_inc(filled.sem, 1)

            def project(layer, b, k, at, m=128):
                fill(layer, b, k, [(wcol(1, layer, at, m), x_hi[:, :]), (wcol(1, layer, at, m), x_lo[:, :]),
                                   (wcol(0, layer, at, m), x_hi[:, :])], m)

            def spread(layer, b, k, sel, n):
                fill(layer, b, k, [(sel, wT[0:n, :])])

            def spread_pair(layer, b, k, pair):
                ring_free(pe, layer, b, k, apart=True)
                for i in range(2):
                    e = 2 * pair + i
                    last = mm(R[k % 3][64 * i:64 * i + 64, :], sel16[:, e:e + 1].to_broadcast([48, 64]), wT[0:48, :],
                              start=True, stop=True)
                last.then_inc(filled.sem, 1)

            def add_unit(layer, b, u, at, rows_=128):
                wait(pe, hi_ok, layer, b, u + 1)
                wait(pe, lo_ok, layer, b, u + 1)
                first = u == 0
                if first and layer != 3:
                    wait(pe, yT_ok, layer, b, 0)
                h, l = h_hi[0:rows_, u % 2, :], h_lo[0:rows_, u % 2, :]
                mm(Y[:, :], wcol(1, layer, at, 128, rows_), h, start=first, stop=False, skip_group_check=True)
                mm(Y[:, :], wcol(1, layer, at, 128, rows_), l, start=False, stop=False, skip_group_check=True)
                last = mm(Y[:, :], wcol(0, layer, at, 128, rows_), h, start=False, stop=u == UNITS[layer] - 1,
                          skip_group_check=True)
                last.then_inc(y_ok.sem, 1)

            def m_unit(layer, b, u):
                if u < UNITS[layer]:
                    uses = RING_OF[layer][u]
                    if layer == 0:
                        if u % 2 == 0:
                            spread(layer, b, uses[0], sel8[:, u // 2:u // 2 + 1].to_broadcast([24, 128]), 24)
                        project(layer, b, uses[-1], u * 128)
                    elif layer == 1:
                        if u < 8:
                            spread_pair(layer, b, uses[0], u)
                            project(layer, b, uses[1], u * 128)
                            project(layer, b, uses[2], 1088 + u * 128)
                        else:
                            project(layer, b, uses[0], 1024, 64)
                            project(layer, b, uses[1], 1088 + 1024, 64)
                    elif layer == 2:
                        if u < 16 and u % 2 == 0:
                            spread(layer, b, uses[0], sel8[:, u // 2:u // 2 + 1].to_broadcast([24, 128]), 24)
                        project(layer, b, uses[-2], u * 128)
                        project(layer, b, uses[-1], 2304 + u * 128)
                    else:
                        fill(layer, b, uses[0], [(sel16[:, u:u + 1].to_broadcast([48, 128]), rsT[:, :])])
                if layer == 3 and 1 <= u <= UNITS[3]:
                    spread(layer, b, RING_OF[3][u - 1][1], sel16[:, u - 1:u].to_broadcast([48, 128]), 48)
                u -= LATE[layer] + 1
                if u < 0:
                    return
                if layer == 0:
                    add_unit(layer, b, u, 2048 + u * 128)
                elif layer == 1:
                    add_unit(layer, b, u, 2176 + u * 128, 128 if u < 8 else 64)
                    if u == 0:
                        for part in (x_hi, x_lo):
                            mm(Y[:, :], ident_ws[:, :], part[:, :], start=False, stop=False, skip_group_check=True)
                elif layer == 2:
                    add_unit(layer, b, u, 4608 + u * 128)
                else:
                    add_unit(layer, b, u, 2048 + u * 128)
                    if u == 0:
                        for part in range(3):
                            mm(Y[:, :], b2_part[:, part, :], wT[:, :], start=False, stop=False, skip_group_check=True)

            def m_pre(layer, b, e):
                if e < 16:
                    project(layer, b, e, e * 128)
                if e == 0:
                    wait(pe, yT_ok, layer, b, 0)
                e -= 2
                if e >= 0:
                    wait(pe, sq_ok, layer, b, e + 1)
                    for t in range(NT):
                        last = mm(Y[:, t * 16 + e:t * 16 + e + 1], hw[:, e % 2, t * 128:t * 128 + 128], mean_col[:, :],
                                  start=True, stop=True)
                    last.then_inc(var_ok.sem, 1)

            def m_mid(layer, b, k):
                wait(pe, rs_ok, layer, b, 6, apart=True)
                to = Y[0:48, :].bitcast(BF16)
                for t in range(NT):
                    last = mm(to[:, t * 128:t * 128 + 128], rs3[:, t, :], ident_bf[:, :], is_transpose=True, start=True, stop=True)
                last.then_inc(rs_tn.sem, 1)
                wait(pe, rs_sv, layer, b, 1)

            def m_end(layer, b, k):
                n = len(RING[layer]) - 1
                wait(pe, yT_ok, layer, b, 1)
                ring_free(pe, layer, b, n)
                for t in range(NT):
                    last = mm(R[n % 3][:, t * 128:t * 128 + 128], yT[:, t * 128:t * 128 + 128], ident, is_transpose=True,
                              start=True, stop=True)
                last.then_inc(filled.sem, 1)

            walk(pe, dict(p_turn=p_turn, p_q=p_q, p_k=p_k, p_v=p_v, q_scores=q_scores,
                          q_turn_a=lambda l, b, t: q_turn(l, b, t, 0), q_turn_b=lambda l, b, t: q_turn(l, b, t, 1),
                          q_pv=q_pv, q_oturn=q_oturn, q_out=q_out, f_turn=f_turn, f_route=f_route, f_wturn=f_wturn,
                          m_start=m_start, m_unit=m_unit, m_pre=m_pre, m_mid=m_mid, m_end=m_end), enter)

        @block.scalar
        def _(sc):
            act_ = nc.scalar.activation
            sc.wait_ge(in_c, 128)
            act_(gate[:, :], bc[:, 520:528], ACT.Tanh).then_inc(c_act, 1)

            def enter(layer):
                if layer == 0:
                    sc.wait_ge(c_dve, 6)

            def w_split(layer, b, k):
                n = MOE_COLS[layer] // PIECES[layer]
                sc.wait_ge(in_w, 16 * (layer + 1))
                w_free(sc, layer)
                if layer == 3:
                    sc.wait_ge(w_cen, 2)
                act_(wcol(1, layer, k * n, n), staging[:, k * n:k * n + n], ACT.Copy, scale=WS).then_inc(w_hi_ok, 1)

            def p_turn(layer, b, k):
                wait(sc, p_xT, layer, b, 1)
                wait(sc, p_qp, layer, b, 0)
                wait(sc, p_kp, layer, b, 0)
                act_(xnT_a[:, :], S[0][:, :], ACT.Copy).then_inc(p_xTs.sem, 1)

            def p_q(layer, b, k):
                wait(sc, p_qp, layer, b, 1)
                wait(sc, q_scr, layer, b, 0)
                act_(q_hl[:, 0, :], S[1][:, :], ACT.Identity, bias=cols[:, 2 * layer:2 * layer + 1]).then_inc(p_qh.sem, 1)

            def p_k(layer, b, k):
                wait(sc, p_kp, layer, b, 1)
                wait(sc, k_scr, layer, b, 0)
                act_(k_hl[:, 0, :], S[0][:, :], ACT.Identity, bias=cols[:, 2 * layer + 1:2 * layer + 2]).then_inc(p_kh.sem, 1)

            def q_exp(layer, b, t):
                wait(sc, s_sub, layer, b, 2 * t + 2)
                act_(prob[:, t, :], prob[:, t, :], ACT.Exp, scale=SCORE_SCALE[layer]).then_inc(e_ok.sem, 1)

            def q_turn_b(layer, b, t):
                wait(sc, pt_ok, layer, b, 2 * t + 2)
                act_(probT[:, t % 2, 4:8, :].rearrange("p j n -> p (j n)"), T[:, :], ACT.Copy).then_inc(pt_b.sem, 1)

            def q_oturn(layer, b, t):
                wait(sc, ot_ok, layer, b, t + 1)
                wait(sc, out_ok, layer, b, t)
                act_(attT[:, :], T[:, 0:128], ACT.Copy).then_inc(ot_sv.sem, 1)

            def f_turn(layer, b, k):
                wait(sc, f_xT, layer, b, 1)
                wait(sc, m_xh, layer, b, 0)
                wait(sc, m_xl, layer, b, 0)
                act_(xnT_f[:, :], A[:, :], ACT.Copy).then_inc(f_xTs.sem, 1)

            def f_route(layer, b, k):
                E = EXPERTS[layer]
                if layer == 1:
                    wait(sc, f_lg, layer, b, 1)
                    wait(sc, rt, layer, b, 0)
                    act_(r_lg[:, :, 0:E], T[:, 0:NT * E].rearrange("p (t e) -> p t e", e=E), ACT.Tanh, scale=0.5)\
                        .then_inc(rt_act.sem, 1)
                else:
                    wait(sc, rt, layer, b, 3)
                    act_(r_ex[:, :, 0:E], r_ex[:, :, 0:E], ACT.Exp).then_inc(rt_act.sem, 1)

            def f_wturn(layer, b, k):
                n = 3 * EXPERTS[layer]
                wait(sc, wt_ok, layer, b, 1)
                wait(sc, m_wc, layer, b, 0)
                act_(wT_next[0:n, :], T[0:n, :].bitcast(BF16)[:, 0:BLK], ACT.Copy).then_inc(wt_sv.sem, 1)

            def m_start(layer, b, k):
                wait(sc, f_xTs, layer, b, 1)
                wait(sc, filled, layer, b, 0)
                wait(sc, y_ok, layer, b, 0)
                act_(x_hi[:, :], xnT_f[:, :], ACT.Copy).then_inc(m_xh.sem, 1)

            def read(layer, b, k, out_, func, m=128, **more):
                wait(sc, filled, layer, b, k + 1)
                act_(out_, R[k % 3][0:m, :], func, **more).then_inc(read_act.sem, 1)

            def m_unit(layer, b, u):
                if u < UNITS[layer]:
                    uses = RING_OF[layer][u]
                    e = u // 2 if layer in (0, 2) else u
                    if layer == 0 and u % 2 == 0:
                        wait(sc, read_dve, layer, b, max(u - 2, 0))
                        read(layer, b, uses[0], w_bc[:, e % 2, :], ACT.Copy, scale=1.0 / WS)
                    elif layer == 1 and u < 8 or layer == 2 and u < 16 and u % 2 == 0:
                        done = u - 1 if layer == 1 else u - 2
                        wait(sc, hw_pool, layer, b, max(done, 0))
                        read(layer, b, uses[0], w_bc[:, e % 2, :], ACT.Copy)
                    if layer in (1, 2):
                        m = 64 if layer == 1 and u == 8 else 128
                        k = uses[-2]
                        wait(sc, read_dve, layer, b, max(u - 1, 0))
                        read(layer, b, k, act[0:m, u % 2, :], ACT.Silu, m, scale=1.0 / WS)
                    if layer == 3:
                        wait(sc, read_dve, layer, b, dve_read(3, uses[0]))
                        act_(had[:, u % 2, :], act[:, u % 2, :], ACT.Gelu, scale=cols[:, 8 + u:9 + u],
                             bias=cols[:, 24 + u:25 + u]).then_inc(gelu_ok.sem, 1)
                u -= LATE[layer]
                if 0 <= u < UNITS[layer]:
                    weighted(sc, layer, b, u)
                    hi_free(sc, layer, b, u)
                    m = 64 if layer == 1 and u == 8 else 128
                    act_(h_hi[0:m, u % 2, :], hw[0:m, u % 2, :], ACT.Copy).then_inc(hi_ok.sem, 1)

            def m_pre(layer, b, e):
                if e < 16:
                    if e == 0:
                        wait(sc, read_dve, layer, b, 0)
                    read(layer, b, e, hidden[:, e, :], ACT.Identity, scale=1.0 / WS, bias=b1_col[:, e:e + 1])

            def m_mid(layer, b, k):
                wait(sc, var_ok, layer, b, 16)
                wait(sc, rs_ok, layer, b, 0)
                act_(sd[:, :, :].rearrange("p t e -> p (t e)"), Y[:, 0:64], ACT.Sqrt, bias=eps_col[:, :]).then_inc(sd_ok.sem, 1)
                wait(sc, rs_tn, layer, b, 1)
                wait(sc, filled, layer, b, 0)
                act_(rsT[:, :], Y[0:48, :].bitcast(BF16)[:, 0:BLK], ACT.Copy).then_inc(rs_sv.sem, 1)

            def m_end(layer, b, k):
                wait(sc, y_ok, layer, b, UNITS[layer])
                wait(sc, filled, layer, b, 0)
                act_(yT[:, :], Y[:, :], ACT.Copy).then_inc(yT_ok.sem, 1)

            walk(sc, dict(w_split=w_split, p_turn=p_turn, p_q=p_q, p_k=p_k, q_exp=q_exp, q_turn_b=q_turn_b,
                          q_oturn=q_oturn, f_turn=f_turn, f_route=f_route, f_wturn=f_wturn, m_start=m_start,
                          m_unit=m_unit, m_pre=m_pre, m_mid=m_mid, m_end=m_end), enter)

        @block.vector
        def _(ve):
            v = nc.vector
            ident = cst[:, 0:128]
            v.memset(ones_bf[:, :], 1.0)
            v.memset(ones_row[:, :], 1.0)
            v.memset(mean_col[:, :], 1.0 / D)
            v.memset(eps_col[:, :], EPS)
            v.memset(carry[:, :], 0.0)
            v.memset(neg_half[:, :], -0.5).then_inc(c_dve, 1)
            ve.wait_ge(in_c, 128)
            v.tensor_copy(ident_bf[:, :], ident)
            v.tensor_scalar(ident_ws[:, :], ident, WS, None, ALU.mult)
            v.tensor_copy(tri[:, :], cst[:, 128:256])
            v.tensor_copy(causal[:, :], cst[:, 256:320])
            v.tensor_copy(sel8[:, :], cst[0:24, 320:328])
            v.tensor_copy(sel16[:, :], cst[0:48, 328:344])
            v.tensor_copy(b2_part[:, 0, :], b2[:, :])
            v.tensor_reduce(b1_mean[:, :], b1[:, :], AX.X, ALU.add).then_inc(c_dve, 1)
            ve.wait_ge(c_dve, 2)
            v.tensor_scalar(b1_mean[:, :], b1_mean[:, :], 1.0 / D, None, ALU.mult)
            v.tensor_tensor(b2_rest[:, 0, :], b2[:, :], b2_part[:, 0, :], ALU.subtract).then_inc(c_dve, 1)
            ve.wait_ge(c_dve, 3)
            v.tensor_copy(b2_part[:, 1, :], b2_rest[:, 0, :])
            v.tensor_scalar(b1[:, :], b1[:, :], b1_mean[:, 0:1], None, ALU.subtract).then_inc(c_dve, 1)
            ve.wait_ge(c_dve, 4)
            v.tensor_tensor(b2_rest[:, 1, :], b2_rest[:, 0, :], b2_part[:, 1, :], ALU.subtract).then_inc(c_dve, 1)
            ve.wait_ge(c_dve, 5)
            v.tensor_scalar(b2_part[:, 2, :], b2_rest[:, 1, :], WS, None, ALU.mult)
            v.tensor_scalar(b2_part[:, 0:2, :], b2_part[:, 0:2, :], WS, None, ALU.mult)
            ve.wait_ge(c_act, 1)
            v.tensor_scalar(gate_ffn[:, :], gate[:, 4:8], 1.0 / WS, None, ALU.mult)
            ve.wait_ge(c_pe, 1)
            v.tensor_copy(b1_col[:, :], A[:, 0:16]).then_inc(c_dve, 1)
            ve.wait_ge(c_dve, 6)

            def enter(layer):
                if layer == 0:
                    ve.wait_ge(in_x[2], 16)

            def w_split(layer, b, k):
                n = MOE_COLS[layer] // PIECES[layer]
                if k == 0 and layer == 3:
                    ve.wait_ge(in_w, 16 * (layer + 1))
                    w1 = staging[:, 0:2048].rearrange("p (e h) -> p e h", h=D)
                    v.tensor_reduce(w_mean[:, :], w1, AX.X, ALU.add).then_inc(w_cen, 1)
                    ve.wait_ge(w_cen, 1)
                    v.scalar_tensor_tensor(out=w1, in0=cast_row(w_mean[:, :], D), scalar=-1.0 / D, in1=w1,
                                           op0=ALU.mult, op1=ALU.add).then_inc(w_cen, 1)
                ve.wait_ge(w_hi_ok, sum(PIECES[:layer]) + k + 1)
                w_free(ve, layer)
                v.scalar_tensor_tensor(out=wcol(0, layer, k * n, n), in0=staging[:, k * n:k * n + n], scalar=WS,
                                       in1=wcol(1, layer, k * n, n), op0=ALU.mult, op1=ALU.subtract).then_inc(w_lo_ok, 1)

            def moments(layer, b, st, mv, stat, mom, var):
                wait(ve, mom, layer, b, 0, apart=True)
                for t in range(NT):
                    last = v.bn_stats(st[:, t, :], tile_x(b, t))
                last.then_inc(stat.sem, 1)
                wait(ve, stat, layer, b, 1, apart=True)
                wait(ve, var, layer, b, 0, apart=True)
                for t in range(NT):
                    last = v.bn_aggr(mv[:, t, :], st[:, t, :])
                last.then_inc(mom.sem, 1)

            def normed(layer, b, xn, mv, r, rstd, done, turned):
                wait(ve, rstd, layer, b, 1)
                wait(ve, turned, layer, b, 0)
                for t in range(NT):
                    last = v.tensor_scalar(xn[:, t, :], tile_x(b, t), mv[:, t, 0:1], r[:, t:t + 1],
                                           ALU.subtract, ALU.mult)
                last.then_inc(done.sem, 1)

            def p_load(layer, b, k):
                if layer == 3:
                    wait(ve, mask_in, layer, b, 16)
                    wait(ve, s_mul, layer, b, 0)
                    v.tensor_scalar(m_mul[:, :, :], m_raw[:, :, :], 0.0, None, ALU.not_equal).then_inc(mask_ok.sem, 1)

            def p_norm(layer, b, k):
                if layer:
                    wait(ve, x_mix, layer - 1, b, 1, apart=True)
                elif isinstance(b, int):
                    ve.wait_ge(in_x[b], 16)
                wait(ve, p_xn, layer, b, 0, apart=True)
                moments(layer, b, p_st, p_mv, p_stat, p_mom, p_var)
                normed(layer, b, xn_a, p_mv, p_rs, p_rstd, p_xn, p_xT)

            def split(layer, b, bank, hl, col, hi, lo, in_dram):
                wait(ve, hi, layer, b, 1)
                wait(ve, in_dram, layer, b, 0)
                v.scalar_tensor_tensor(out=hl[:, 1, :], in0=bank[:, :], scalar=cols[:, col:col + 1], in1=hl[:, 0, :],
                                       op0=ALU.add, op1=ALU.subtract).then_inc(lo.sem, 1)

            def p_q(layer, b, k):
                split(layer, b, S[1], q_hl, 2 * layer, p_qh, p_ql, q_scr)

            def p_k(layer, b, k):
                split(layer, b, S[0], k_hl, 2 * layer + 1, p_kh, p_kl, k_scr)

            def p_v(layer, b, k):
                wait(ve, pv_ok, layer, b, 0)
                if layer == 0 and isinstance(b, int) and b == 0:
                    ve.wait_ge(c_pool, 3)
                bv = bc[:, layer * D:layer * D + D].rearrange("p (j h d) -> p j h d", j=8, h=2)
                for t in range(NT):
                    if t % 2 == 0:
                        wait(ve, p_vp, layer, b, t // 2 + 1)
                    src = S[t // 2][:, (t % 2) * 256:(t % 2) * 256 + 256].rearrange("p (b j h d) -> p b j h d", b=2, j=8, h=2)
                    for h in range(2):
                        for e in range(2):
                            r = slice(64 * h, 64 * h + 64)
                            last = v.tensor_tensor(v_diag[r, t, :, e, h, 0:HD], src[r, e, :, h, :], bv[r, :, h, :], ALU.add)
                last.then_inc(p_vd.sem, 1)

            def q_scores(layer, b, t):
                wait(ve, pt_ok, layer, b, 0)
                for half in range(2):
                    n = 2 * t + half + 1
                    s = S[half][:, :].rearrange("p (h k) -> p h k", h=8)
                    p = prob[:, t, half * 512:half * 512 + 512].rearrange("p (h k) -> p h k", h=8)
                    mx = q_mx[:, half, :]
                    wait(ve, s_ok, layer, b, n)
                    if layer == 3:
                        v.tensor_tensor(p, s, m_mul[:, t, :].unsqueeze(1).to_broadcast([128, 8, SEQ]), ALU.mult)\
                            .then_inc(s_mul.sem, 1)
                        wait(ve, s_mul, layer, b, n)
                        s = p
                    wait(ve, s_sub, layer, b, max(n - 2, 0))
                    v.tensor_reduce(mx, s, AX.X, ALU.max).then_inc(s_max.sem, 1)
                    wait(ve, s_max, layer, b, n)
                    if layer == 3:
                        v.scalar_tensor_tensor(out=p, in0=p, scalar=1e-20, in1=cast_row(mx, SEQ), op0=ALU.add,
                                               op1=ALU.subtract).then_inc(s_sub.sem, 1)
                    else:
                        v.tensor_tensor(p, s, cast_row(mx, SEQ), ALU.subtract).then_inc(s_sub.sem, 1)

            def q_turn_a(layer, b, t):
                wait(ve, pt_ok, layer, b, 2 * t + 1)
                wait(ve, pv_ok, layer, b, max(t - 1, 0))
                v.tensor_copy(probT[:, t % 2, 0:4, :].rearrange("p j n -> p (j n)"), T[:, :]).then_inc(pt_a.sem, 1)

            def q_pv(layer, b, t):
                wait(ve, pv_ok, layer, b, t + 1)
                wait(ve, o_ok, layer, b, t)
                a = A[:, 0:288].rearrange("p (j b h d) -> p j b h d", j=8, b=2, h=2)
                for e in range(2):
                    r = slice(64 * e, 64 * e + 64)
                    last = v.reciprocal(q_rc[r, :, :], a[r, :, e, :, HD])
                last.then_inc(rc_ok.sem, 1)
                wait(ve, rc_ok, layer, b, t + 1)
                wait(ve, ot_ok, layer, b, t)
                for e in range(2):
                    r = slice(64 * e, 64 * e + 64)
                    last = v.tensor_tensor(att[r, :].rearrange("p (j h d) -> p j h d", j=8, h=2), a[r, :, e, :, 0:HD],
                                           q_rc[r, :, :].unsqueeze(3).to_broadcast([64, 8, 2, HD]), ALU.mult)
                last.then_inc(o_ok.sem, 1)

            def q_out(layer, b, t):
                wait(ve, out_ok, layer, b, t + 1)
                x = tile_x(b, t)
                v.scalar_tensor_tensor(out=x, in0=A[:, 0:128], scalar=gate[:, layer:layer + 1], in1=x,
                                       op0=ALU.mult, op1=ALU.add).then_inc(x_att.sem, 1)

            def f_norm(layer, b, k):
                wait(ve, x_att, layer, b, 4, apart=True)
                wait(ve, f_xn, layer, b, 0, apart=True)
                moments(layer, b, f_st, f_mv, f_stat, f_mom, f_var)
                normed(layer, b, xn_f, f_mv, f_rs, f_rstd, f_xn, f_xT)

            def f_route(layer, b, k):
                E = EXPERTS[layer]
                step = [0]

                def then(ins, wait_apart=False):
                    step[0] += 1
                    ins.then_inc(rt.sem, 1)
                    wait(ve, rt, layer, b, step[0], wait_apart)

                lg, ex, val, key = r_lg[:, :, 0:E], r_ex[:, :, 0:E], r_val[:, :, 0:E], r_key[:, :, 0:E]
                oh, w, w2 = r_oh[:, :, :, 0:E], r_w[:, :, 0:E], r_w2[:, :, 0:E]
                wait(ve, f_lg, layer, b, 1)
                if layer == 1:
                    wait(ve, rt_act, layer, b, 1, apart=layer == 0)
                    then(v.tensor_scalar(val, lg, 0.5, 0.5, ALU.mult, ALU.add), True)
                    key = val
                else:
                    then(v.tensor_copy(lg, T[:, 0:NT * E].rearrange("p (t e) -> p t e", e=E)))
                    then(v.tensor_reduce(r_s[:, 0, :], lg, AX.X, ALU.max))
                    then(v.tensor_tensor(ex, lg, cast_row(r_s[:, 0, :], E), ALU.subtract), True)
                    wait(ve, rt_act, layer, b, 1, apart=layer == 0)
                    if layer == 0:
                        val, key = ex, lg
                    else:
                        then(v.tensor_reduce(r_s[:, 1, :], ex, AX.X, ALU.add))
                        then(v.reciprocal(r_s[:, 2, :], r_s[:, 1, :]))
                        then(v.tensor_tensor(val, ex, cast_row(r_s[:, 2, :], E), ALU.mult), True)
                        if layer == 2:
                            gb = bc[:, 512:520].unsqueeze(1).to_broadcast([128, NT, E])
                            then(v.tensor_tensor(key, val, gb, ALU.add), True)
                        else:
                            key = val
                for t in range(NT):
                    last = v.max(r_top[:, t, :], key[:, t, :])
                then(last, True)
                for t in range(NT):
                    last = v.max_index(r_idx[:, t, :], r_top[:, t, :], key[:, t, :])
                then(last)
                then(v.tensor_copy(r_idf[:, :, :], r_idx[:, :, :]))
                iota = cst[:, 344:344 + E].unsqueeze(1).to_broadcast([128, NT, E])
                v.tensor_tensor(oh[:, 0], iota, cast_row(r_idf[:, :, 0], E), ALU.is_equal)
                then(v.tensor_tensor(oh[:, 1], iota, cast_row(r_idf[:, :, 1], E), ALU.is_equal))
                then(v.tensor_tensor(w, oh[:, 0], oh[:, 1], ALU.add))
                then(v.tensor_tensor(w2, w, val, ALU.mult))
                if layer != 2:
                    then(v.tensor_reduce(r_s[:, 3, :], w2, AX.X, ALU.add))
                    if layer == 3:
                        then(v.tensor_scalar(r_s[:, 3, :], r_s[:, 3, :], 1e-9, None, ALU.max))
                    then(v.reciprocal(r_s[:, 1, :], r_s[:, 3, :]))
                    then(v.tensor_tensor(w, w2, cast_row(r_s[:, 1, :], E), ALU.mult))
                    w, w2 = w2, w
                if layer == 0:
                    then(v.tensor_scalar(r_one[:, :, :], w2, 0.0, None, ALU.is_gt))
                    then(v.tensor_reduce(r_sum[:, :], r_one[:, :, :].rearrange("p t e -> p e t"), AX.X, ALU.add))
                    wait(ve, cum_ok, layer, b, 1)
                    then(v.scalar_tensor_tensor(out=w, in0=A[:, 0:NT * E].rearrange("p (t e) -> p t e", e=E),
                                                scalar=float(CAPACITY), in1=w2, op0=ALU.is_le, op1=ALU.mult))
                    then(v.tensor_tensor(carry[:, :], carry[:, :], r_sum[:, :], ALU.add))
                    w, w2 = w2, w
                parts = w3[:, :, 0:3 * E].rearrange("p t (k e) -> p t k e", k=3)
                rest = r_rest[:, :, :, 0:E]
                wait(ve, wt_ok, layer, b, 0)
                then(v.tensor_copy(parts[:, :, 0, :], w2))
                then(v.tensor_tensor(rest[:, 0], w2, parts[:, :, 0, :], ALU.subtract))
                then(v.tensor_copy(parts[:, :, 1, :], rest[:, 0]))
                then(v.tensor_tensor(rest[:, 1], rest[:, 0], parts[:, :, 1, :], ALU.subtract))
                v.tensor_copy(parts[:, :, 2, :], rest[:, 1]).then_inc(w3_ok.sem, 1)
                assert step[0] == ROUTE_STEPS[layer]

            def m_start(layer, b, k):
                wait(ve, m_xh, layer, b, 1)
                wait(ve, filled, layer, b, 0)
                wait(ve, y_ok, layer, b, 0)
                v.tensor_tensor(x_lo[:, :], xnT_f[:, :], x_hi[:, :], ALU.subtract).then_inc(m_xl.sem, 1)

            def hw_free(layer, b, u):
                wait(ve, hi_ok, layer, b, max(u - 1, 0))
                wait(ve, lo_ok, layer, b, max(u - 1, 0))

            def m_unit(layer, b, u):
                if u < UNITS[layer]:
                    k = RING_OF[layer][u][-1]
                    bank = R[k % 3]
                    if layer == 0:
                        wait(ve, filled, layer, b, k + 1)
                        wait(ve, read_act, layer, b, u // 2 + 1)
                        hw_free(layer, b, u)
                        v.scalar_tensor_tensor(out=hw[:, u % 2, :], in0=bank[:, :], scalar=0.0,
                                               in1=w_bc[:, u // 2 % 2, :], op0=ALU.max, op1=ALU.mult).then_inc(read_dve.sem, 1)
                    elif layer in (1, 2):
                        pool = HW_POOL[layer]
                        m = 64 if layer == 1 and u == 8 else 128
                        wait(ve, filled, layer, b, k + 1)
                        wait(ve, read_act, layer, b, act_read(layer, k - 1))
                        if u < pool:
                            wait(ve, hw_pool, layer, b, max(u - 1, 0))
                            to = had
                        else:
                            wait(ve, hw_pool, layer, b, pool)
                            hw_free(layer, b, u)
                            to = hw
                        v.scalar_tensor_tensor(out=to[0:m, u % 2, :], in0=bank[0:m, :], scalar=1.0 / WS,
                                               in1=act[0:m, u % 2, :], op0=ALU.mult, op1=ALU.mult).then_inc(read_dve.sem, 1)
                    else:
                        k = RING_OF[3][u][0]
                        wait(ve, filled, layer, b, k + 1)
                        wait(ve, read_act, layer, b, u + 1)
                        wait(ve, gelu_ok, layer, b, max(u - 1, 0))
                        v.tensor_tensor(act[:, u % 2, :], hidden[:, u, :], R[k % 3][:, :], ALU.mult).then_inc(read_dve.sem, 1)
                u -= 1
                if not 0 <= u < UNITS[layer]:
                    return
                if layer == 3:
                    k = RING_OF[3][u][1]
                    wait(ve, filled, layer, b, k + 1)
                    wait(ve, gelu_ok, layer, b, u + 1)
                    hw_free(layer, b, u)
                    v.tensor_tensor(hw[:, u % 2, :], had[:, u % 2, :], R[k % 3][:, :], ALU.mult).then_inc(read_dve.sem, 1)
                elif layer in (1, 2):
                    lo_part(ve, layer, b, u)

            def m_mid(layer, b, k):
                parts = rs3[:, :, :].rearrange("p t (k e) -> p t k e", k=3)
                wait(ve, sd_ok, layer, b, 1)
                wait(ve, rs_tn, layer, b, 0)
                steps_ = [lambda: v.reciprocal(rs[:, :, :], sd[:, :, :]),
                          lambda: v.tensor_copy(parts[:, :, 0, :], rs[:, :, :]),
                          lambda: v.tensor_tensor(rs_rest[:, 0], rs[:, :, :], parts[:, :, 0, :], ALU.subtract),
                          lambda: v.tensor_copy(parts[:, :, 1, :], rs_rest[:, 0]),
                          lambda: v.tensor_tensor(rs_rest[:, 1], rs_rest[:, 0], parts[:, :, 1, :], ALU.subtract),
                          lambda: v.tensor_copy(parts[:, :, 2, :], rs_rest[:, 1])]
                for n, step in enumerate(steps_):
                    step().then_inc(rs_ok.sem, 1)
                    wait(ve, rs_ok, layer, b, n + 1)

            def m_end(layer, b, k):
                n = len(RING[layer]) - 1
                wait(ve, filled, layer, b, n + 1)
                x = tile_x(b, 0, NT)
                v.scalar_tensor_tensor(out=x, in0=R[n % 3][:, :], scalar=gate_ffn[:, layer:layer + 1], in1=x,
                                       op0=ALU.mult, op1=ALU.add).then_inc(x_mix.sem, 1)

            walk(ve, dict(w_split=w_split, p_load=p_load, p_norm=p_norm, p_q=p_q, p_k=p_k, p_v=p_v, q_scores=q_scores,
                          q_turn_a=q_turn_a, q_pv=q_pv, q_out=q_out, f_norm=f_norm, f_route=f_route, m_start=m_start,
                          m_unit=m_unit, m_mid=m_mid, m_end=m_end), enter)

        @block.gpsimd
        def _(gp):
            g = nc.gpsimd
            g.memset(k_diag[:, :, :, :], 0.0).then_inc(c_pool, 1)
            g.memset(v_diag[:, :, :, :, :, :], 0.0).then_inc(c_pool, 1)
            gp.wait_ge(c_pool, 2)
            for h in range(2):
                last = g.memset(v_diag[64 * h:64 * h + 64, :, :, :, h, HD:HD + 1], 1.0)
            last.then_inc(c_pool, 1)
            gp.wait_ge(c_pool, 3)
            gp.wait_ge(c_dve, 1)

            def rstd(layer, b, mv, ve_, r, mom, var, out_, normed):
                wait(gp, mom, layer, b, 1, apart=True)
                wait(gp, out_, layer, b, 0, apart=True)
                g.tensor_scalar(ve_[:, :], mv[:, :, 1], EPS, None, ALU.add).then_inc(var.sem, 1)
                wait(gp, var, layer, b, 1)
                wait(gp, normed, layer, b, 0)
                g.tensor_tensor(r[:, :], ve_[:, :], neg_half[:, :], ALU.pow).then_inc(out_.sem, 1)

            def p_load(layer, b, k):
                if layer in (0, 2):
                    wait(gp, mask_in, layer, b, 16 if layer == 0 else 32, apart=True)
                    wait(gp, s_ok, layer, b, 0, apart=True)
                    g.tensor_scalar(m_add[:, :, :], m_raw[:, :, :], 0.0, MASKED, ALU.is_equal, ALU.mult)\
                        .then_inc(mask_ok.sem, 1)

            def p_norm(layer, b, k):
                rstd(layer, b, p_mv, p_ve, p_rs, p_mom, p_var, p_rstd, p_xn)

            def f_norm(layer, b, k):
                rstd(layer, b, f_mv, f_ve, f_rs, f_mom, f_var, f_rstd, f_xn)

            def m_start(layer, b, k):
                n = 3 * EXPERTS[layer]
                wait(gp, wt_sv, layer, b, 1, apart=True)
                wait(gp, filled, layer, b, 0, apart=True)
                wait(gp, y_ok, layer, b, 0, apart=True)
                g.tensor_copy(wT[0:n, :], wT_next[0:n, :]).then_inc(m_wc.sem, 1)

            def m_pre(layer, b, e):
                if e < 16:
                    wait(gp, read_act, layer, b, e + 1)
                    if e < 2:
                        wait(gp, hi_ok, layer, b, 0)
                        wait(gp, lo_ok, layer, b, 0)
                    else:
                        wait(gp, var_ok, layer, b, e - 1)
                    g.tensor_tensor(hw[:, e % 2, :], hidden[:, e, :], hidden[:, e, :], ALU.mult).then_inc(sq_ok.sem, 1)

            def m_unit(layer, b, u):
                if layer in (1, 2) and u < HW_POOL[layer]:
                    e = u // 2 if layer == 2 else u
                    wait(gp, read_dve, layer, b, u + 1)
                    wait(gp, hi_ok, layer, b, max(u - 1, 0))
                    wait(gp, lo_ok, layer, b, max(u - 1, 0))
                    g.tensor_tensor(hw[:, u % 2, :], had[:, u % 2, :], w_bc[:, e % 2, :], ALU.mult).then_inc(hw_pool.sem, 1)
                u -= LATE[layer]
                if layer in (0, 3) and 0 <= u < UNITS[layer]:
                    lo_part(g, layer, b, u)

            walk(gp, dict(p_load=p_load, p_norm=p_norm, f_norm=f_norm, m_start=m_start, m_pre=m_pre, m_unit=m_unit),
                 lambda layer: None)


def kernel(**inputs):
    import numpy as np
    import concourse.bacc as bacc
    from concourse.bass_utils import run_bass_kernel_spmd

    a = {k: np.asarray(x) for k, x in inputs.items()}
    f = np.float32

    def T(x):
        return np.ascontiguousarray(np.swapaxes(x, -1, -2))

    def flat(x):
        return np.transpose(x, (1, 0, 2)).reshape(x.shape[1], -1)

    def chunks(x):
        return np.transpose(x.reshape(x.shape[0], 2, 128, -1), (2, 0, 1, 3)).reshape(128, -1)

    att = [[T(a[f"L{i}_xattn_W{w}"]) for w in "qkvo"] for i in range(LAYERS)]
    w_att = flat(np.stack([w for layer in att for w in layer]))
    l1_down = a["L1_ffn_experts_wd"].reshape(8, 128, D)
    shared_down = np.concatenate([a["L1_ffn_shared_wd"], np.zeros((64, D), f)])
    l2 = {w: np.concatenate([a[f"L2_ffn_w{w}"], a[f"L2_ffn_sw{w}"][None]]) for w in "123"}
    w_moe = np.concatenate([
        flat(T(a["L0_ffn_first_linear"])), chunks(T(a["L0_ffn_second_linear"])),
        flat(a["L1_ffn_experts_wg"]), a["L1_ffn_shared_wg"], flat(a["L1_ffn_experts_wu"]), a["L1_ffn_shared_wu"],
        flat(l1_down), shared_down,
        flat(T(l2["1"])), flat(T(l2["3"])), chunks(T(l2["2"])),
        flat(a["L3_ffn_W1"]), flat(a["L3_ffn_W2"])], axis=1)
    w_rt = np.concatenate([T(a["L0_ffn_expert_embeddings"]), a["L1_ffn_gate_w"], T(a["L2_ffn_gate_w"]), a["L3_ffn_Wr"]], axis=1)
    rows = np.concatenate([a["L0_xattn_bo"], a["L2_xattn_bo"], a["L3_xattn_bo"], a["L1_ffn_gate_b"], a["L3_ffn_br"]])[None]
    none = np.zeros(D, f)
    cols = np.stack([none] * 4 + [a["L2_xattn_bq"], a["L2_xattn_bk"], a["L3_xattn_bq"], a["L3_xattn_bk"]], axis=1)
    cols = np.concatenate([cols, T(a["L3_ffn_g1"]), T(a["L3_ffn_be1"])], axis=1)
    bc = np.concatenate([none, none, a["L2_xattn_bv"], a["L3_xattn_bv"], a["L2_ffn_gate_bias"], a["g_xattn"], a["g_ffn"]])[None]
    causal = np.tile(np.where(np.tril(np.ones((SEQ, SEQ), bool)), 0.0, MASKED), (2, 1))
    row = np.arange(128)[:, None]
    cst = np.concatenate([np.eye(128), np.triu(np.ones((128, 128))), causal, row % 8 == np.arange(8)[None],
                          row % 16 == np.arange(16)[None], np.tile(np.arange(16), (128, 1))], axis=1).astype(f)
    m2 = np.transpose(a["mask_BxS2_ik0"].reshape(NB, NT, 2, SEQ), (0, 2, 1, 3)).reshape(NB, 2, NT * SEQ)
    arrays = {
        "x": a["x"].reshape(TOK, D), "ctxT": T(a["ctx_1024"].reshape(TOK, D)),
        "m0": a["mask_Bx1xSxS2_if1"].reshape(TOK, SEQ), "m2": m2, "m3": a["mask_Bx1xSxS2_ik1"].reshape(TOK, SEQ),
        "w_att": w_att, "w_moe": w_moe, "w_rt": w_rt, "rows": rows, "cols": cols, "bc": bc,
        "b1": a["L3_ffn_b1"], "b2": np.concatenate([a["L3_ffn_b2"]] * 3), "cst": cst,
    }
    arrays = {f"{k}_dram": np.ascontiguousarray(x) for k, x in arrays.items()}
    nc = bacc.Bacc("TRN2", target_bir_lowering=False, num_devices=1, dynamic_dma_scratch_size=1024)
    args = [nc.dram_tensor(k, x.shape, mybir.dt.from_np(x.dtype), kind="ExternalInput").ap() for k, x in arrays.items()]
    out = nc.dram_tensor("out_dram", (TOK, D), F32, kind="ExternalOutput").ap()
    build(nc, *args, out)
    r = run_bass_kernel_spmd(nc, [arrays], core_ids=[0])
    return r.results[0]["out_dram"].reshape(BATCH, SEQ, D)
```

```python
from contextlib import ExitStack

import concourse.bass as bass
from concourse import mybir

F32, F16, BF16 = mybir.dt.float32, mybir.dt.float16, mybir.dt.bfloat16
I32, U32 = mybir.dt.int32, mybir.dt.uint32
ALU, ACT, AX = mybir.AluOpType, mybir.ActivationFunctionType, mybir.AxisListType

LAYERS, D, HEADS, HD, SEQ, BATCH = 4, 128, 16, 8, 64, 128
TOK = BATCH * SEQ
TILE = 128
NT = 4
BLK = NT * TILE
NB = TOK // BLK
EXPERTS = [8, 16, 8, 16]
CAPACITY = -(-TOK // EXPERTS[0])
EPS = 1e-5
MASKED = -1e20
WS = 64.0
SCORE_SCALE = [HD ** -0.5, HD ** -0.5, HD ** -0.5, D ** -0.5]
MOE_COLS = [4096, 3328, 6912, 4096]
MOE_BASE = [sum(MOE_COLS[:i]) for i in range(LAYERS)]
W_AT = [0, MOE_COLS[2], 0, MOE_COLS[2]]
W_COLS = MOE_COLS[2] + MOE_COLS[3]
PIECES = [4, 4, 6, 4]
HI_FIRST = [False, False, False, True]
UNITS = [16, 9, 18, 16]
ROUTE_STEPS = [20, 14, 17, 20]
HW_POOL = [0, 8, 16, 0]
LATE = [1, 1, 1, 2]


def ring_plan(layer):
    if layer == 0:
        uses = [True, False, False] * 8
    elif layer == 1:
        uses = [True, True, False] * 8 + [True, False]
    elif layer == 2:
        uses = ([True] + [True, False] * 2) * 8 + [True, False] * 2
    else:
        uses = [True] * 16 + [False, False] * 16
    return uses + [False]


RING = [ring_plan(layer) for layer in range(LAYERS)]
RING_ACT = [sum(r) for r in RING]
RING_DVE = [len(r) - sum(r) - 1 for r in RING]
RING_OF = [
    [[3 * (u // 2)] * (u % 2 == 0) + [3 * (u // 2) + 1 + u % 2] for u in range(16)],
    [[3 * u, 3 * u + 1, 3 * u + 2] if u < 8 else [24, 25] for u in range(9)],
    [([5 * (u // 2)] * (u % 2 == 0) + [5 * (u // 2) + 1 + 2 * (u % 2), 5 * (u // 2) + 2 + 2 * (u % 2)])
     if u < 16 else [40 + 2 * (u - 16), 41 + 2 * (u - 16)] for u in range(18)],
    [[15 + 2 * u if u else 16, min(18 + 2 * u, 47)] for u in range(16)],
]


AT = [
    {
        "m_go": 0.03, "m_sum": 0.2933, "m_bend": 1.4, "m_lag_sc": 0.0066, "m_lag_ve": 0.0, "m_lag_gp": 0.0,
        "q_lag": 0, "f_stats": 0.0, "f_norm": 0.04, "f_turn": 0.08, "f_logits": 0.12, "f_exp": 0.2,
        "f_pick": 0.265, "f_count": 0.383, "f_parts": 0.386, "f_wturn": 0.398, "q_scores": 0.0005,
        "scores_each": 0.0514, "q_exp": 0.205, "exp_each": 0, "tile_each": 0.1639, "q_turn_a": 0.2482,
        "q_turn_b": 0.2765, "q_pv": 0.3082, "q_oturn": 0.3482, "q_out": 0.3782, "p_load": 0.02, "p_mask": 0.205,
        "p_stats": 0.3, "p_norm": 0.34, "p_turn": 0.38, "p_q": 0.43, "p_k": 0.5, "p_v": 0.93,
    },
    {
        "m_go": 0.03, "m_sum": 0.5, "m_bend": 1.0, "m_lag_sc": 0.1899, "m_lag_ve": 0.4, "m_lag_gp": 0.3117,
        "q_lag": 0, "f_stats": 0.0, "f_norm": 0.04, "f_turn": 0.08, "f_logits": 0.12, "f_exp": 0.1905,
        "f_pick": 0.2376, "f_count": 0.3629, "f_parts": 0.3637, "f_wturn": 0.3744, "q_scores": 0.001,
        "scores_each": 0.0702, "q_exp": 0.2218, "exp_each": 0, "tile_each": 0.1536, "q_turn_a": 0.2317,
        "q_turn_b": 0.2617, "q_pv": 0.2973, "q_oturn": 0.3337, "q_out": 0.3621, "p_load": 0.02, "p_mask": 0.2218,
        "p_stats": 0.23, "p_norm": 0.27, "p_turn": 0.31, "p_q": 0.365, "p_k": 0.43, "p_v": 0.93,
    },
    {
        "m_go": 0.03, "m_sum": 0.5, "m_bend": 1.0, "m_lag_sc": 0.2, "m_lag_ve": 0.4, "m_lag_gp": 0.4, "q_lag": 0,
        "f_stats": 0.0, "f_norm": 0.0456, "f_turn": 0.08, "f_logits": 0.12, "f_exp": 0.2, "f_pick": 0.22,
        "f_count": 0.4098, "f_parts": 0.4106, "f_wturn": 0.4114, "q_scores": 0.0125, "scores_each": 0.0524,
        "q_exp": 0.205, "exp_each": 0, "tile_each": 0.1917, "q_turn_a": 0.279, "q_turn_b": 0.3102, "q_pv": 0.339,
        "q_oturn": 0.379, "q_out": 0.409, "p_load": 0.0548, "p_mask": 0.205, "p_stats": 0.3, "p_norm": 0.34,
        "p_turn": 0.38, "p_q": 0.43, "p_k": 0.5, "p_v": 0.93,
    },
    {
        "m_go": 0.0, "m_sum": 0.2055, "m_bend": 1.0, "m_lag_sc": 0.0, "m_lag_ve": 0.0, "m_lag_gp": 0.0,
        "q_lag": 0, "m_mid": 0.42, "mid_gap": 0.05, "pre_lag_sc": 0, "pre_lag_gp": 0, "f_stats": 0.0,
        "f_norm": 0.0213, "f_turn": 0.08, "f_logits": 0.12, "f_exp": 0.1476, "f_pick": 0.25, "f_count": 0.3648,
        "f_parts": 0.3656, "f_wturn": 0.3798, "q_scores": 0.001, "scores_each": 0.0503, "q_exp": 0.205,
        "exp_each": 0, "tile_each": 0.1748, "q_turn_a": 0.2058, "q_turn_b": 0.2267, "q_pv": 0.2567,
        "q_oturn": 0.2967, "q_out": 0.333, "p_load": 0.02, "p_mask": 0.205, "p_stats": 0.3, "p_norm": 0.34,
        "p_turn": 0.38, "p_q": 0.43, "p_k": 0.5, "p_v": 0.93,
    },
]


def turn(engine, mix, route, attend, prepare, split=None):
    steps = []
    at = AT[mix[0] if mix else 0]

    def step(when, name, where, k=0):
        steps.append((when, name, *where, k))

    if mix:
        layer = mix[0]
        step(-0.001, "m_start", mix)
        first = at["m_go"]
        if layer == 3:
            n = EXPERTS[3] + 2
            each = (at["m_mid"] - first) / n
            for e in range(n):
                step(first + each * (e + at.get("pre_lag_" + engine, 0)), "m_pre", mix, e)
            step(at["m_mid"] + each, "m_mid", mix)
            first = at["m_mid"] + at["mid_gap"]
        n = UNITS[layer] + LATE[layer] + 1
        for u in range(n):
            for name, lag in ("m_unit", at.get("m_lag_" + engine, 0)), ("m_sum", at["m_sum"]):
                step(first + (0.98 - first) * ((u + lag) / n) ** at["m_bend"], name, mix, u)
        step(0.985, "m_end", mix)
    if route:
        for name in ("f_stats", "f_norm", "f_turn", "f_logits", "f_exp", "f_pick", "f_count", "f_parts", "f_wturn"):
            step(at[name], name, route, attend)
    if attend:
        for t in range(NT):
            step(at["q_scores"] + at["scores_each"] * t, "q_scores", attend, t)
            step(at["q_exp"] + at["exp_each"] * t, "q_exp", attend, t)
            for name in ("q_turn_a", "q_turn_b", "q_pv", "q_oturn", "q_out"):
                lag = at["q_lag"] * (engine in ("sc", "ve") and name != "q_turn_b")
                step(at[name] + at["tile_each"] * t + lag, name, attend, t)
    if prepare:
        for name in ("p_load", "p_mask", "p_stats", "p_norm", "p_turn", "p_q", "p_k", "p_v"):
            step(at[name], name, prepare)
    if split is not None:
        for i in range(PIECES[split]):
            step(0.2 + 0.1 * i, "w_split", (split, 0), i)
    steps.sort(key=lambda s: s[0])
    return [s[1:] for s in steps]


def walk(engine, eng, steps, enter):

    def run(sequence):
        for name, layer, b, k in sequence:
            if name in steps:
                steps[name](layer, b, k)

    run([("w_split", 0, 0, i) for i in range(PIECES[0])])
    run(turn(engine, None, None, None, (0, 0)))
    run(turn(engine, None, None, (0, 0), (0, 1)))
    run(turn(engine, None, (0, 0), (0, 1), (0, 2)))
    for layer in range(LAYERS):

        def at(b):
            if b < NB:
                return layer, b
            return (layer + 1, b - NB) if layer + 1 < LAYERS else None

        enter(layer)
        run(turn(engine, (layer, 0), (layer, 1), (layer, 2), (layer, 3)))
        with eng.Fori(1, NB - 3) as i:
            run(turn(engine, (layer, i), (layer, i + 1), (layer, i + 2), (layer, i + 3)))
        for b in range(NB - 3, NB):
            run(turn(engine, at(b), at(b + 1), at(b + 2), at(b + 3),
                     layer + 1 if b == NB - 3 and layer + 1 < LAYERS else None))


class Signal:

    def __init__(self, sem, per_block):
        self.sem = sem
        self.n = per_block if isinstance(per_block, list) else [per_block] * LAYERS
        self.base = [NB * sum(self.n[:i]) for i in range(LAYERS)]

    def count(self, layer, b, k):
        return b * self.n[layer] + (self.base[layer] + k)


def build(nc, x_in, ctx_in, m0_in, m2_in, m3_in, watt_in, wmoe_in, wrt_in, rows_in, cols_in, bc_in,
          b1_in, b2_in, cst_in, out):
    scratch_q = nc.dram_tensor("scratch_q", (4, 128, BLK), F16).ap()
    scratch_k = nc.dram_tensor("scratch_k", (4, 128, BLK), F16).ap()

    with ExitStack() as ctx:
        def sb(name, shape, dt=F32):
            return ctx.enter_context(nc.sbuf_tensor(name, shape, dt))

        def sem(name):
            return ctx.enter_context(nc.semaphore(name))

        def signal(name, per_block=1):
            return Signal(sem(name), per_block)

        xs = sb("xs", [128, NB * NT * D])
        w_hi = sb("w_hi", [128, W_COLS], F16)
        w_lo = sb("w_lo", [128, W_COLS], F16)
        w_att = sb("w_att", [128, LAYERS, 4, D])
        w_rt = sb("w_rt", [128, 48])
        rows = sb("rows", [1, 416])
        cols = sb("cols", [128, 40])
        bc = sb("bc", [128, LAYERS * D + 8 + 8])
        cst = sb("cst", [128, 376])
        b1 = sb("b1", [16, D])
        b2 = sb("b2", [48, D])
        gate = sb("gate", [128, 8])
        gate_ffn = sb("gate_ffn", [128, 4])
        ident_bf = sb("ident_bf", [128, 128], BF16)
        ident_ws = sb("ident_ws", [128, 128], F16)
        tri = sb("tri", [128, 128], BF16)
        ones_bf = sb("ones_bf", [128, 128], BF16)
        ones_row = sb("ones_row", [1, 128])
        mean_at = sb("mean_at", [128, 31])
        eps_col = sb("eps_col", [128, 1])
        neg_half = sb("neg_half", [128, NT])
        causal = sb("causal", [128, SEQ], BF16)
        sel8 = sb("sel8", [24, 8], BF16)
        sel16 = sb("sel16", [48, 16], BF16)
        sel_rs = sb("sel_rs", [80, 16], BF16)
        b1_col = sb("b1_col", [128, 16])
        b1_mean = sb("b1_mean", [16, 1])
        b2_part = sb("b2_part", [48, 3, D], BF16)
        w_mean = sb("w_mean", [128, 16])
        hidden = sb("hidden", [128, 16, BLK])
        staging = hidden[:, :, :].rearrange("p e n -> p (e n)")
        ctxT = sb("ctxT", [128, BLK])
        m_raw = sb("m_raw", [128, NT, SEQ], I32)
        m_add = sb("m_add", [128, NT, SEQ], BF16)
        m_mul = sb("m_mul", [128, NT, SEQ])
        p_st = sb("p_st", [128, NT, 6])
        p_mv = sb("p_mv", [128, NT, 2])
        p_ve = sb("p_ve", [128, NT])
        p_rs = sb("p_rs", [128, NT])
        xn_a = sb("xn_a", [128, NT, D])
        xnT_a = sb("xnT_a", [128, BLK])
        q_hl = sb("q_hl", [128, 2, BLK], F16)
        k_hl = sb("k_hl", [128, 2, BLK], F16)
        q_stack = sb("q_stack", [128, 4, BLK], F16)
        k_diag = sb("k_diag", [128, 4, 4, BLK], F16)
        v_diag = sb("v_diag", [128, NT, 8, 2, 2, HD + 1])
        prob = sb("prob", [128, NT, HEADS * SEQ])
        q_mx = sb("q_mx", [128, 2, 8])
        probT = sb("probT", [128, 2, 8, TILE])
        q_rc = sb("q_rc", [128, 8, 2])
        att = sb("att", [128, D])
        attT = sb("attT", [128, TILE])
        f_st = sb("f_st", [128, NT, 6])
        f_mv = sb("f_mv", [128, NT, 2])
        f_ve = sb("f_ve", [128, NT])
        f_rs = sb("f_rs", [128, NT])
        xn_f = sb("xn_f", [128, NT, D])
        xnT_f = sb("xnT_f", [128, BLK])
        r_lg = sb("r_lg", [128, NT, 16])
        r_ex = sb("r_ex", [128, NT, 16])
        r_val = sb("r_val", [128, NT, 16])
        r_key = sb("r_key", [128, NT, 16])
        r_oh = sb("r_oh", [128, 2, NT, 16])
        r_w = sb("r_w", [128, NT, 16])
        r_w2 = sb("r_w2", [128, NT, 16])
        r_rest = sb("r_rest", [128, 2, NT, 16])
        r_top = sb("r_top", [128, NT, 8])
        r_idx = sb("r_idx", [128, NT, 8], U32)
        r_idf = sb("r_idf", [128, NT, 8])
        r_s = sb("r_s", [128, 4, NT])
        r_one = sb("r_one", [128, NT, 8], BF16)
        r_sum = sb("r_sum", [128, 8])
        carry = sb("carry", [128, 8], BF16)
        w3 = sb("w3", [128, NT, 48], BF16)
        wT_next = sb("wT_next", [48, BLK], BF16)
        wT = sb("wT", [48, BLK], BF16)
        x_hi = sb("x_hi", [128, BLK], F16)
        x_lo = sb("x_lo", [128, BLK], F16)
        w_bc = sb("w_bc", [128, 2, BLK])
        act = sb("act", [128, 2, BLK])
        had = sb("had", [128, 2, BLK])
        hw = sb("hw", [128, 2, BLK])
        h_hi = sb("h_hi", [128, 2, BLK], F16)
        h_lo = sb("h_lo", [128, 2, BLK], F16)
        yT = sb("yT", [128, BLK])
        b2_rest = yT[0:48, 0:2 * D].rearrange("p (k d) -> p k d", k=2)
        rsT = sb("rsT", [80, BLK], BF16)

        ps = [ctx.enter_context(nc.psum_tensor(f"ps{i}", [128, 512], F32)) for i in range(8)]
        S, A, T, R, Y = ps[0:2], ps[2], ps[3], ps[4:7], ps[7]

        in_x = [sem("x_loaded_0"), sem("x_loaded_1"), sem("x_loaded_2"), sem("x_loaded_rest")]
        in_c = sem("constants_loaded")
        in_w = sem("expert_weights_loaded")
        w_hi_ok, w_lo_ok, w_cen = sem("w_hi_ready"), sem("w_lo_ready"), sem("w_centred")
        c_dve, c_pool, c_act, c_pe = sem("consts_dve"), sem("consts_pool"), sem("consts_act"), sem("consts_pe")
        stored = sem("out_stored")
        ctx_ok = signal("ctx_loaded", 16)
        mask_in = signal("mask_loaded", [16, 0, 32, 16])
        mask_ok = signal("mask_ready", [1, 0, 1, 1])
        p_stat, p_mom, p_var, p_rstd = signal("p_stats"), signal("p_moments"), signal("p_var_eps"), signal("p_rstd")
        p_xn, p_xT, p_xTs = signal("p_normed"), signal("p_turned"), signal("p_xT_saved")
        p_qp, p_kp = signal("q_projected"), signal("k_projected")
        p_qh, p_ql, p_kh, p_kl = signal("q_hi"), signal("q_lo"), signal("k_hi"), signal("k_lo")
        q_scr, k_scr, q_ok, k_ok = signal("q_in_dram", 64), signal("k_in_dram", 64), signal("q_stacked", 16), signal("k_stacked", 64)
        p_vp, p_vd = signal("v_projected", 2), signal("v_placed")
        s_ok = signal("scores_ready", 8)
        s_mul = signal("scores_masked", [0, 0, 0, 8])
        s_max, s_sub = signal("scores_max", 8), signal("scores_shifted", 8)
        e_ok = signal("exp_ready", 4)
        pt_ok, pt_a, pt_b = signal("probs_turned", 8), signal("probT_a_saved", 4), signal("probT_b_saved", 4)
        pv_ok, rc_ok, o_ok = signal("pv_ready", 4), signal("sums_inverted", 4), signal("att_ready", 4)
        ot_ok, ot_sv, out_ok, x_att = signal("att_turned", 4), signal("attT_saved", 4), signal("att_projected", 4), signal("x_attended", 4)
        f_stat, f_mom, f_var, f_rstd = signal("f_stats"), signal("f_moments"), signal("f_var_eps"), signal("f_rstd")
        f_xn, f_xT, f_xTs, f_lg = signal("f_normed"), signal("f_turned"), signal("f_xT_saved"), signal("logits_ready")
        rt = signal("route_step", ROUTE_STEPS)
        rt_act = signal("route_act", 1)
        cum_ok = signal("cumsum_ready", [1, 0, 0, 0])
        w3_ok, wt_ok, wt_sv = signal("weights_split"), signal("weights_turned"), signal("wT_saved")
        m_xh, m_xl, m_wc = signal("x_hi_ready"), signal("x_lo_ready"), signal("wT_copied")
        filled = signal("ring_filled", [len(r) for r in RING])
        read_act, read_dve = signal("ring_read_act", RING_ACT), signal("ring_read_dve", RING_DVE)
        hw_pool = signal("hidden_weighted", HW_POOL)
        hi_ok = signal("hidden_hi", UNITS)
        lo_ok = signal("hidden_lo", UNITS)
        y_ok = signal("unit_added", UNITS)
        gelu_ok = signal("gelu_ready", [0, 0, 0, 16])
        sq_ok, var_ok = signal("squares_ready", [0, 0, 0, 16]), signal("variances_ready", [0, 0, 0, 16])
        sd_ok, rs_ok = signal("sd_ready", [0, 0, 0, 1]), signal("rstd_split", [0, 0, 0, 6])
        yT_ok, x_mix = signal("yT_saved"), signal("x_mixed")

        def wait(eng, sig, layer, b, k, apart=False):
            value = sig.count(layer, b, k)
            if not (isinstance(value, int) and value <= 0):
                if apart and not isinstance(value, int):
                    value = eng.to_reg(value)
                    eng.wait_ge(c_dve, 1)
                eng.wait_ge(sig.sem, value)

        def tile_x(b, t, n=1):
            return xs[:, bass.ds((b * NT + t) * D, n * D)]

        def cast_row(ap, n):
            return ap.unsqueeze(2).to_broadcast([ap.shape[0], ap.shape[1], n])

        def wcol(hi, layer, at, n, rows_=128):
            w = w_hi if hi else w_lo
            return w[0:rows_, W_AT[layer] + at:W_AT[layer] + at + n]

        def w_free(eng, layer):
            if layer >= 2:
                wait(eng, y_ok, layer - 1, 0, 0)

        def ring_free(eng, layer, b, k, apart=False):
            if k == 0:
                wait(eng, x_mix, layer, b, 0, apart)
            elif k >= 3:
                by_act = RING[layer][k - 3]
                nth = sum(1 for r in RING[layer][:k - 2] if r == by_act)
                wait(eng, read_act if by_act else read_dve, layer, b, nth, apart)

        def act_read(layer, k):
            return sum(RING[layer][:k + 1])

        def dve_read(layer, k):
            return k + 1 - sum(RING[layer][:k + 1])

        def weighted(eng, layer, b, u):
            if u < HW_POOL[layer]:
                wait(eng, hw_pool, layer, b, u + 1)
            else:
                wait(eng, read_dve, layer, b, dve_read(layer, RING_OF[layer][u][-1]))

        def hi_free(eng, layer, b, u):
            wait(eng, y_ok, layer, b, max(u - 1, 0))

        def lo_part(eng, layer, b, u):
            m = 64 if layer == 1 and u == 8 else 128
            weighted(eng, layer, b, u)
            wait(eng, hi_ok, layer, b, u + 1)
            wait(eng, y_ok, layer, b, max(u - 1, 0))
            eng.tensor_tensor(h_lo[0:m, u % 2, :], hw[0:m, u % 2, :], h_hi[0:m, u % 2, :], ALU.subtract)\
               .then_inc(lo_ok.sem, 1)

        block = ctx.enter_context(nc.Block())

        @block.sync
        def _(sp):
            def load_x(n, b0, b1_):
                sp.dma_start(xs[:, b0 * NT * D:b1_ * NT * D].rearrange("p (t d) -> p t d", d=D),
                             x_in[b0 * BLK:b1_ * BLK, :].rearrange("(t p) d -> p t d", p=128)).then_inc(in_x[n], 16)

            load_x(0, 0, 1)
            sp.dma_start(cst[:, :], cst_in).then_inc(in_c, 16)
            sp.dma_start(w_att[:, :, :, :].rearrange("p a b c -> p (a b c)"), watt_in).then_inc(in_c, 16)
            sp.dma_start(cols[:, :], cols_in).then_inc(in_c, 16)
            sp.dma_start(bc[:, :], bc_in[0, :].partition_broadcast(128)).then_inc(in_c, 16)
            sp.dma_start(rows[:, :], rows_in).then_inc(in_c, 16)
            sp.dma_start(w_rt[:, :], wrt_in).then_inc(in_c, 16)
            sp.dma_start(b1[:, :], b1_in).then_inc(in_c, 16)
            sp.dma_start(b2[:, :], b2_in).then_inc(in_c, 16)
            load_x(1, 1, 2)
            load_x(2, 2, 3)

            def w_split(layer, b, k):
                if k == 0:
                    if layer:
                        sp.wait_ge(w_lo_ok, sum(PIECES[:layer]))
                        sp.wait_ge(w_hi_ok, sum(PIECES[:layer]))
                    sp.dma_start(staging[:, 0:MOE_COLS[layer]],
                                 wmoe_in[:, MOE_BASE[layer]:MOE_BASE[layer] + MOE_COLS[layer]]).then_inc(in_w, 16)

            def p_load(layer, b, k):
                wait(sp, p_vp, layer, b, 0, apart=True)
                wait(sp, p_kp, layer, b, 0, apart=True)
                sp.dma_start(ctxT[:, :], ctx_in[:, bass.ds(b * BLK, BLK)]).then_inc(ctx_ok.sem, 16)
                if layer == 1:
                    return
                wait(sp, mask_ok, layer, b, 0, apart=True)
                if layer == 2:
                    for half in range(2):
                        sp.dma_start(m_raw[64 * half:64 * half + 64, :, :].rearrange("p (o t) k -> p o (t k)", o=1),
                                     m2_in[bass.ds(b, 1), half, :].partition_broadcast(64))\
                            .then_inc(mask_in.sem, 16)
                else:
                    src = m0_in if layer == 0 else m3_in
                    sp.dma_start(m_raw[:, :, :], src[bass.ds(b * BLK, BLK), :].rearrange("(t p) k -> p t k", p=128))\
                        .then_inc(mask_in.sem, 16)

            def stack(layer, b, src, lo_signal, parts, scratch, in_dram):
                wait(sp, lo_signal, layer, b, 1, apart=True)
                to = scratch.rearrange("g (j t p) n -> t (g j) p n", j=4, t=4)
                for t in range(4):
                    sp.dma_start(to[t], src[:, parts[t], :]).then_inc(in_dram.sem, 16)
                wait(sp, in_dram, layer, b, 64, apart=True)

            def p_q(layer, b, k):
                stack(layer, b, q_hl, p_ql, (0, 0, 1, 1), scratch_q, q_scr)
                wait(sp, s_ok, layer, b, 0, apart=True)
                sp.dma_start(q_stack[:, :, :], scratch_q.rearrange("g p n -> p g n")).then_inc(q_ok.sem, 16)
                wait(sp, q_ok, layer, b, 16, apart=True)

            def p_k(layer, b, k):
                stack(layer, b, k_hl, p_kl, (0, 1, 0, 1), scratch_k, k_scr)
                wait(sp, s_ok, layer, b, 0, apart=True)
                if layer == 0 and isinstance(b, int) and b == 0:
                    sp.wait_ge(c_pool, 1)
                for j in range(4):
                    sp.dma_start(k_diag[32 * j:32 * j + 32, j, :, :],
                                 scratch_k[:, 32 * j:32 * j + 32, :].rearrange("g p n -> p g n")).then_inc(k_ok.sem, 16)
                wait(sp, k_ok, layer, b, 64, apart=True)

            def m_end(layer, b, k):
                if layer == LAYERS - 1:
                    wait(sp, x_mix, layer, b, 1, apart=True)
                    sp.dma_start(out[bass.ds(b * BLK, BLK), :].rearrange("(t p) d -> p t d", p=128),
                                 tile_x(b, 0, NT).rearrange("p (t d) -> p t d", d=D)).then_inc(stored, 16)

            def enter(layer):
                if layer == 0:
                    load_x(3, 3, NB)

            walk("sp", sp, dict(w_split=w_split, p_load=p_load, p_q=p_q, p_k=p_k, m_end=m_end), enter)
            sp.wait_ge(stored, 16 * NB)

        @block.tensor
        def _(pe):
            mm = nc.tensor.matmul
            ident = cst[:, 0:128]
            pe.wait_ge(in_c, 128)
            pe.wait_ge(c_dve, 5)
            mm(A[:, 0:16], b1[:, :], ident[0:16, 0:16], is_transpose=True, start=True, stop=True).then_inc(c_pe, 1)
            pe.wait_ge(c_dve, 6)

            def enter(layer):
                pe.wait_ge(w_hi_ok, sum(PIECES[:layer + 1]))
                pe.wait_ge(w_lo_ok, sum(PIECES[:layer + 1]))

            def p_turn(layer, b, k):
                wait(pe, p_xn, layer, b, 1)
                wait(pe, s_sub, layer, b, 0)
                for t in range(NT):
                    last = mm(S[0][:, t * 128:t * 128 + 128], xn_a[:, t, :], ident, is_transpose=True, start=True, stop=True)
                last.then_inc(p_xT.sem, 1)

            def p_q(layer, b, k):
                wait(pe, ctx_ok, layer, b, 16)
                wait(pe, p_xTs, layer, b, 1)
                mm(S[1][:, :], w_att[:, layer, 0, :], xnT_a[:, :],
                   start=True, stop=True).then_inc(p_qp.sem, 1)

            def p_k(layer, b, k):
                mm(S[0][:, :], w_att[:, layer, 1, :], ctxT[:, :],
                   start=True, stop=True).then_inc(p_kp.sem, 1)

            def p_v(layer, b, k):
                for half, free in ((0, p_kl), (1, p_ql)):
                    wait(pe, free, layer, b, 1)
                    for i in range(4):
                        tb = 4 * half + i
                        for copy in range(2):
                            last = mm(S[half][64 * copy:64 * copy + 64, i * 128:i * 128 + 128],
                                      ctxT[:, 64 * tb:64 * tb + 64], w_att[:, layer, 2, :], start=True, stop=True)
                    last.then_inc(p_vp.sem, 1)

            def q_scores(layer, b, t):
                if t == 0:
                    wait(pe, q_ok, layer, b, 16)
                    wait(pe, k_ok, layer, b, 64)
                    wait(pe, p_vd, layer, b, 1)
                    if layer != 1:
                        wait(pe, mask_ok, layer, b, 1)
                for half in range(2):
                    if t:
                        wait(pe, s_sub, layer, b, 2 * t - 1 + half)
                    if layer != 3:
                        m = causal[:, :] if layer == 1 else m_add[:, t, :]
                        mm(S[half][:, :].rearrange("p (h k) -> p h k", h=8), ident_bf[:, :],
                           m.unsqueeze(1).to_broadcast([128, 8, SEQ]), start=True, stop=False, skip_group_check=True)
                    for g in (2 * half, 2 * half + 1):
                        for e in range(2):
                            at = t * TILE + e * SEQ
                            last = mm(S[half][64 * e:64 * e + 64, (g % 2) * 256:(g % 2) * 256 + 256].rearrange("p (j k) -> p j k", j=4),
                                      q_stack[:, g, at:at + SEQ], k_diag[:, :, g, at:at + SEQ],
                                      start=(layer == 3), stop=True, skip_group_check=True)
                    last.then_inc(s_ok.sem, 1)

            def q_turn(layer, b, t, half):
                if half == 0:
                    wait(pe, e_ok, layer, b, t + 1)
                    wait(pe, ot_sv, layer, b, t)
                    if t == 0:
                        wait(pe, rt_act, layer, b, 0)
                    elif t == 1:
                        wait(pe, wt_sv, layer, b, 0)
                else:
                    wait(pe, pt_a, layer, b, t + 1)
                for i in range(4):
                    j = 4 * half + i
                    last = mm(T[:, i * 128:i * 128 + 128], prob[:, t, j * 128:j * 128 + 128], ident,
                              is_transpose=True, start=True, stop=True)
                last.then_inc(pt_ok.sem, 1)

            def q_pv(layer, b, t):
                wait(pe, pt_a, layer, b, t + 1)
                wait(pe, pt_b, layer, b, t + 1)
                if t == 0:
                    wait(pe, f_xTs, layer, b, 0)
                else:
                    wait(pe, x_att, layer, b, t)
                    if t == 1:
                        wait(pe, rt, layer, b, 0)
                for j in range(8):
                    last = mm(A[:, 36 * j:36 * j + 36], probT[:, t % 2, j, :],
                              v_diag[:, t, j, :, :, :].rearrange("p b h d -> p (b h d)"), start=True, stop=True)
                last.then_inc(pv_ok.sem, 1)

            def q_oturn(layer, b, t):
                wait(pe, o_ok, layer, b, t + 1)
                wait(pe, pt_b, layer, b, t + 1)
                mm(T[:, 0:128], att[:, :], ident, is_transpose=True, start=True, stop=True).then_inc(ot_ok.sem, 1)

            def q_out(layer, b, t):
                wait(pe, ot_sv, layer, b, t + 1)
                row = {0: 0, 2: 128, 3: 256}.get(layer)
                last = mm(A[:, 0:128], attT[:, :], w_att[:, layer, 3, :], start=True, stop=row is None)
                if row is not None:
                    last = mm(A[:, 0:128], ones_row[:, :], rows[:, row:row + 128], start=False, stop=True)
                last.then_inc(out_ok.sem, 1)

            def f_turn(layer, b, k):
                wait(pe, f_xn, layer, b, 1)
                wait(pe, x_att, layer, b, 4)
                for t in range(NT):
                    last = mm(A[:, t * 128:t * 128 + 128], xn_f[:, t, :], ident, is_transpose=True, start=True, stop=True)
                last.then_inc(f_xT.sem, 1)

            def f_logits(layer, b, k):
                E = EXPERTS[layer]
                at = (0, 8, 24, 32)[layer]
                row = {1: 384, 3: 400}.get(layer)
                wait(pe, f_xTs, layer, b, 1)
                wait(pe, ot_sv, layer, b, 4)
                for t in range(NT):
                    last = mm(T[:, t * E:t * E + E], xnT_f[:, t * 128:t * 128 + 128], w_rt[:, at:at + E],
                              start=True, stop=row is None)
                    if row is not None:
                        last = mm(T[:, t * E:t * E + E], ones_row[:, :], rows[:, row:row + E], start=False, stop=True)
                last.then_inc(f_lg.sem, 1)

            def f_count(layer, b, attend):
                if layer == 0:
                    if attend:
                        wait(pe, x_att, *attend, 1)
                    wait(pe, rt, 0, b, 13)
                    for t in range(NT):
                        o = A[:, 8 * t:8 * t + 8]
                        mm(o, tri[:, :], r_one[:, t, :], start=True, stop=False)
                        for s in range(t):
                            mm(o, ones_bf[:, :], r_one[:, s, :], start=False, stop=False)
                        last = mm(o, ones_bf[:, :], carry[:, :], start=False, stop=True)
                    last.then_inc(cum_ok.sem, 1)

            def f_wturn(layer, b, attend):
                n = 3 * EXPERTS[layer]
                if attend:
                    wait(pe, ot_sv, *attend, 1, apart=True)
                wait(pe, w3_ok, layer, b, 1, apart=True)
                to = T[0:n, :].bitcast(BF16)
                for t in range(NT):
                    last = mm(to[:, t * 128:t * 128 + 128], w3[:, t, 0:n], ident_bf[:, :], is_transpose=True, start=True, stop=True)
                last.then_inc(wt_ok.sem, 1)

            def fill(layer, b, k, pairs, m=128):
                ring_free(pe, layer, b, k)
                for n, (lhs, rhs) in enumerate(pairs):
                    last = mm(R[k % 3][0:m, :], lhs, rhs, start=(n == 0), stop=(n == len(pairs) - 1))
                last.then_inc(filled.sem, 1)

            def project(layer, b, k, at, m=128):
                fill(layer, b, k, [(wcol(1, layer, at, m), x_hi[:, :]), (wcol(1, layer, at, m), x_lo[:, :]),
                                   (wcol(0, layer, at, m), x_hi[:, :])], m)

            def spread(layer, b, k, sel, n):
                fill(layer, b, k, [(sel, wT[0:n, :])])

            def spread_pair(layer, b, k, pair):
                ring_free(pe, layer, b, k, apart=True)
                for i in range(2):
                    e = 2 * pair + i
                    last = mm(R[k % 3][64 * i:64 * i + 64, :], sel16[:, e:e + 1].to_broadcast([48, 64]), wT[0:48, :],
                              start=True, stop=True)
                last.then_inc(filled.sem, 1)

            def add_unit(layer, b, u, at, rows_=128):
                wait(pe, hi_ok, layer, b, u + 1)
                wait(pe, lo_ok, layer, b, u + 1)
                first = u == 0
                if first and layer != 3:
                    wait(pe, yT_ok, layer, b, 0)
                h, l = h_hi[0:rows_, u % 2, :], h_lo[0:rows_, u % 2, :]
                mm(Y[:, :], wcol(1, layer, at, 128, rows_), h, start=first, stop=False, skip_group_check=True)
                mm(Y[:, :], wcol(1, layer, at, 128, rows_), l, start=False, stop=False, skip_group_check=True)
                last = mm(Y[:, :], wcol(0, layer, at, 128, rows_), h, start=False, stop=u == UNITS[layer] - 1,
                          skip_group_check=True)
                last.then_inc(y_ok.sem, 1)

            def m_unit(layer, b, u):
                if u == 0:
                    wait(pe, m_wc, layer, b, 1)
                    wait(pe, m_xl, layer, b, 1)
                if u < UNITS[layer]:
                    uses = RING_OF[layer][u]
                    if layer == 0:
                        if u % 2 == 0:
                            spread(layer, b, uses[0], sel8[:, u // 2:u // 2 + 1].to_broadcast([24, 128]), 24)
                        project(layer, b, uses[-1], u * 128)
                    elif layer == 1:
                        if u < 8:
                            spread_pair(layer, b, uses[0], u)
                            project(layer, b, uses[1], u * 128)
                            project(layer, b, uses[2], 1088 + u * 128)
                        else:
                            project(layer, b, uses[0], 1024, 64)
                            project(layer, b, uses[1], 1088 + 1024, 64)
                    elif layer == 2:
                        if u < 16 and u % 2 == 0:
                            spread(layer, b, uses[0], sel8[:, u // 2:u // 2 + 1].to_broadcast([24, 128]), 24)
                        project(layer, b, uses[-2], u * 128)
                        project(layer, b, uses[-1], 2304 + u * 128)
                    else:
                        fill(layer, b, uses[0], [(sel_rs[:, u:u + 1].to_broadcast([80, 128]), rsT[:, :])])
                if layer == 3 and 1 <= u <= UNITS[3]:
                    spread(layer, b, RING_OF[3][u - 1][1], sel16[:, u - 1:u].to_broadcast([48, 128]), 48)

            def m_sum(layer, b, u):
                u -= LATE[layer] + 1
                if u < 0:
                    return
                if layer == 0:
                    add_unit(layer, b, u, 2048 + u * 128)
                elif layer == 1:
                    add_unit(layer, b, u, 2176 + u * 128, 128 if u < 8 else 64)
                    if u == 0:
                        for part in (x_hi, x_lo):
                            mm(Y[:, :], ident_ws[:, :], part[:, :], start=False, stop=False, skip_group_check=True)
                elif layer == 2:
                    add_unit(layer, b, u, 4608 + u * 128)
                else:
                    add_unit(layer, b, u, 2048 + u * 128)
                    if u == 0:
                        for part in range(3):
                            mm(Y[:, :], b2_part[:, part, :], wT[:, :], start=False, stop=False, skip_group_check=True)

            def m_pre(layer, b, e):
                if e == 0:
                    wait(pe, m_xl, layer, b, 1)
                if e < 16:
                    project(layer, b, e, e * 128)
                if e == 0:
                    wait(pe, yT_ok, layer, b, 0)
                e -= 2
                if e >= 0:
                    wait(pe, sq_ok, layer, b, e + 1)
                    mm(Y[0:16, :], mean_at[:, 15 - e:31 - e], hw[:, e % 2, :], start=e == 0, stop=e == 15,
                       skip_group_check=True).then_inc(var_ok.sem, 1)

            def m_mid(layer, b, k):
                wait(pe, rs_ok, layer, b, 6)

            def m_end(layer, b, k):
                n = len(RING[layer]) - 1
                wait(pe, yT_ok, layer, b, 1)
                ring_free(pe, layer, b, n)
                for t in range(NT):
                    last = mm(R[n % 3][:, t * 128:t * 128 + 128], yT[:, t * 128:t * 128 + 128], ident, is_transpose=True,
                              start=True, stop=True)
                last.then_inc(filled.sem, 1)

            walk("pe", pe, dict(p_turn=p_turn, p_q=p_q, p_k=p_k, p_v=p_v, q_scores=q_scores,
                          q_turn_a=lambda l, b, t: q_turn(l, b, t, 0), q_turn_b=lambda l, b, t: q_turn(l, b, t, 1),
                          q_pv=q_pv, q_oturn=q_oturn, q_out=q_out, f_turn=f_turn, f_logits=f_logits, f_count=f_count, f_wturn=f_wturn,
                          m_unit=m_unit, m_sum=m_sum, m_pre=m_pre, m_mid=m_mid, m_end=m_end), enter)

        @block.scalar
        def _(sc):
            act_ = nc.scalar.activation
            sc.wait_ge(in_c, 128)
            act_(gate[:, :], bc[:, 520:528], ACT.Tanh).then_inc(c_act, 1)

            def enter(layer):
                if layer == 0:
                    sc.wait_ge(c_dve, 6)

            def w_split(layer, b, k):
                n = MOE_COLS[layer] // PIECES[layer]
                sc.wait_ge(in_w, 16 * (layer + 1))
                w_free(sc, layer)
                if layer == 3:
                    sc.wait_ge(w_cen, 2)
                act_(wcol(1, layer, k * n, n), staging[:, k * n:k * n + n], ACT.Copy, scale=WS).then_inc(w_hi_ok, 1)

            def p_turn(layer, b, k):
                wait(sc, p_xT, layer, b, 1)
                wait(sc, p_qp, layer, b, 0)
                wait(sc, p_kp, layer, b, 0)
                act_(xnT_a[:, :], S[0][:, :], ACT.Copy).then_inc(p_xTs.sem, 1)

            def p_q(layer, b, k):
                wait(sc, p_qp, layer, b, 1)
                wait(sc, q_scr, layer, b, 0)
                act_(q_hl[:, 0, :], S[1][:, :], ACT.Identity, bias=cols[:, 2 * layer:2 * layer + 1]).then_inc(p_qh.sem, 1)

            def p_k(layer, b, k):
                wait(sc, p_kp, layer, b, 1)
                wait(sc, k_scr, layer, b, 0)
                act_(k_hl[:, 0, :], S[0][:, :], ACT.Identity, bias=cols[:, 2 * layer + 1:2 * layer + 2]).then_inc(p_kh.sem, 1)

            def q_exp(layer, b, t):
                wait(sc, s_sub, layer, b, 2 * t + 2)
                act_(prob[:, t, :], prob[:, t, :], ACT.Exp, scale=SCORE_SCALE[layer]).then_inc(e_ok.sem, 1)

            def q_turn_b(layer, b, t):
                wait(sc, pt_ok, layer, b, 2 * t + 2)
                act_(probT[:, t % 2, 4:8, :].rearrange("p j n -> p (j n)"), T[:, :], ACT.Copy).then_inc(pt_b.sem, 1)

            def q_oturn(layer, b, t):
                wait(sc, ot_ok, layer, b, t + 1)
                wait(sc, out_ok, layer, b, t)
                act_(attT[:, :], T[:, 0:128], ACT.Copy).then_inc(ot_sv.sem, 1)

            def f_turn(layer, b, k):
                wait(sc, f_xT, layer, b, 1)
                wait(sc, m_xh, layer, b, 0)
                wait(sc, m_xl, layer, b, 0)
                act_(xnT_f[:, :], A[:, :], ACT.Copy).then_inc(f_xTs.sem, 1)

            def f_exp(layer, b, k):
                E = EXPERTS[layer]
                if layer == 1:
                    wait(sc, f_lg, layer, b, 1)
                    wait(sc, rt, layer, b, 0)
                    act_(r_lg[:, :, 0:E], T[:, 0:NT * E].rearrange("p (t e) -> p t e", e=E), ACT.Tanh, scale=0.5)\
                        .then_inc(rt_act.sem, 1)
                else:
                    wait(sc, rt, layer, b, 3)
                    act_(r_ex[:, :, 0:E], r_ex[:, :, 0:E], ACT.Exp).then_inc(rt_act.sem, 1)

            def f_wturn(layer, b, k):
                n = 3 * EXPERTS[layer]
                wait(sc, wt_ok, layer, b, 1)
                wait(sc, m_wc, layer, b, 0)
                act_(wT_next[0:n, :], T[0:n, :].bitcast(BF16)[:, 0:BLK], ACT.Copy).then_inc(wt_sv.sem, 1)

            def m_start(layer, b, k):
                wait(sc, f_xTs, layer, b, 1)
                wait(sc, filled, layer, b, 0)
                wait(sc, y_ok, layer, b, 0)
                act_(x_hi[:, :], xnT_f[:, :], ACT.Copy).then_inc(m_xh.sem, 1)

            def read(layer, b, k, out_, func, m=128, **more):
                wait(sc, filled, layer, b, k + 1)
                act_(out_, R[k % 3][0:m, :], func, **more).then_inc(read_act.sem, 1)

            def high(layer, b, u):
                if 0 <= u < UNITS[layer]:
                    weighted(sc, layer, b, u)
                    hi_free(sc, layer, b, u)
                    m = 64 if layer == 1 and u == 8 else 128
                    act_(h_hi[0:m, u % 2, :], hw[0:m, u % 2, :], ACT.Copy).then_inc(hi_ok.sem, 1)

            def m_unit(layer, b, u):
                if HI_FIRST[layer]:
                    high(layer, b, u - LATE[layer])
                if u < UNITS[layer]:
                    uses = RING_OF[layer][u]
                    e = u // 2 if layer in (0, 2) else u
                    if layer == 0 and u % 2 == 0:
                        wait(sc, read_dve, layer, b, max(u - 2, 0))
                        read(layer, b, uses[0], w_bc[:, e % 2, :], ACT.Copy, scale=1.0 / WS)
                    elif layer == 1 and u < 8 or layer == 2 and u < 16 and u % 2 == 0:
                        done = u - 1 if layer == 1 else u - 2
                        wait(sc, hw_pool, layer, b, max(done, 0))
                        read(layer, b, uses[0], w_bc[:, e % 2, :], ACT.Copy)
                    if layer in (1, 2):
                        m = 64 if layer == 1 and u == 8 else 128
                        k = uses[-2]
                        wait(sc, read_dve, layer, b, max(u - 1, 0))
                        read(layer, b, k, act[0:m, u % 2, :], ACT.Silu, m, scale=1.0 / WS)
                    if layer == 3:
                        wait(sc, read_dve, layer, b, dve_read(3, uses[0]))
                        act_(had[:, u % 2, :], act[:, u % 2, :], ACT.Gelu, scale=cols[:, 8 + u:9 + u],
                             bias=cols[:, 24 + u:25 + u]).then_inc(gelu_ok.sem, 1)
                if not HI_FIRST[layer]:
                    high(layer, b, u - LATE[layer])

            def m_pre(layer, b, e):
                if e < 16:
                    if e == 0:
                        wait(sc, read_dve, layer, b, 0)
                    read(layer, b, e, hidden[:, e, :], ACT.Identity, scale=1.0 / WS, bias=b1_col[:, e:e + 1])

            def m_mid(layer, b, k):
                wait(sc, var_ok, layer, b, 16)
                wait(sc, gelu_ok, layer, b, 0)
                wait(sc, read_dve, layer, b, 0)
                act_(act[0:16, 0, :], Y[0:16, :], ACT.Sqrt, bias=eps_col[0:16, :]).then_inc(sd_ok.sem, 1)

            def m_end(layer, b, k):
                wait(sc, y_ok, layer, b, UNITS[layer])
                wait(sc, filled, layer, b, 0)
                act_(yT[:, :], Y[:, :], ACT.Copy).then_inc(yT_ok.sem, 1)

            walk("sc", sc, dict(w_split=w_split, p_turn=p_turn, p_q=p_q, p_k=p_k, q_exp=q_exp, q_turn_b=q_turn_b,
                          q_oturn=q_oturn, f_turn=f_turn, f_exp=f_exp, f_wturn=f_wturn, m_start=m_start,
                          m_unit=m_unit, m_pre=m_pre, m_mid=m_mid, m_end=m_end), enter)

        @block.vector
        def _(ve):
            v = nc.vector
            ident = cst[:, 0:128]
            v.memset(ones_bf[:, :], 1.0)
            v.memset(ones_row[:, :], 1.0)
            v.memset(mean_at[:, 0:15], 0.0)
            v.memset(mean_at[:, 15:16], 1.0 / D)
            v.memset(mean_at[:, 16:31], 0.0)
            v.memset(rsT[:, :], 0.0)
            v.memset(eps_col[:, :], EPS)
            v.memset(carry[:, :], 0.0)
            v.memset(neg_half[:, :], -0.5).then_inc(c_dve, 1)
            ve.wait_ge(in_c, 128)
            v.tensor_copy(ident_bf[:, :], ident)
            v.tensor_scalar(ident_ws[:, :], ident, WS, None, ALU.mult)
            v.tensor_copy(tri[:, :], cst[:, 128:256])
            v.tensor_copy(causal[:, :], cst[:, 256:320])
            v.tensor_copy(sel8[:, :], cst[0:24, 320:328])
            v.tensor_copy(sel16[:, :], cst[0:48, 328:344])
            v.tensor_copy(sel_rs[:, :], cst[0:80, 360:376])
            v.tensor_copy(b2_part[:, 0, :], b2[:, :])
            v.tensor_reduce(b1_mean[:, :], b1[:, :], AX.X, ALU.add).then_inc(c_dve, 1)
            ve.wait_ge(c_dve, 2)
            v.tensor_scalar(b1_mean[:, :], b1_mean[:, :], 1.0 / D, None, ALU.mult)
            v.tensor_tensor(b2_rest[:, 0, :], b2[:, :], b2_part[:, 0, :], ALU.subtract).then_inc(c_dve, 1)
            ve.wait_ge(c_dve, 3)
            v.tensor_copy(b2_part[:, 1, :], b2_rest[:, 0, :])
            v.tensor_scalar(b1[:, :], b1[:, :], b1_mean[:, 0:1], None, ALU.subtract).then_inc(c_dve, 1)
            ve.wait_ge(c_dve, 4)
            v.tensor_tensor(b2_rest[:, 1, :], b2_rest[:, 0, :], b2_part[:, 1, :], ALU.subtract).then_inc(c_dve, 1)
            ve.wait_ge(c_dve, 5)
            v.tensor_scalar(b2_part[:, 2, :], b2_rest[:, 1, :], WS, None, ALU.mult)
            v.tensor_scalar(b2_part[:, 0:2, :], b2_part[:, 0:2, :], WS, None, ALU.mult)
            ve.wait_ge(c_act, 1)
            v.tensor_scalar(gate_ffn[:, :], gate[:, 4:8], 1.0 / WS, None, ALU.mult)
            ve.wait_ge(c_pe, 1)
            v.tensor_copy(b1_col[:, :], A[:, 0:16]).then_inc(c_dve, 1)
            ve.wait_ge(c_dve, 6)

            def enter(layer):
                if layer == 0:
                    ve.wait_ge(in_x[3], 16)

            def w_split(layer, b, k):
                n = MOE_COLS[layer] // PIECES[layer]
                if k == 0 and layer == 3:
                    ve.wait_ge(in_w, 16 * (layer + 1))
                    w1 = staging[:, 0:2048].rearrange("p (e h) -> p e h", h=D)
                    v.tensor_reduce(w_mean[:, :], w1, AX.X, ALU.add).then_inc(w_cen, 1)
                    ve.wait_ge(w_cen, 1)
                    v.scalar_tensor_tensor(out=w1, in0=cast_row(w_mean[:, :], D), scalar=-1.0 / D, in1=w1,
                                           op0=ALU.mult, op1=ALU.add).then_inc(w_cen, 1)
                ve.wait_ge(w_hi_ok, sum(PIECES[:layer]) + k + 1)
                w_free(ve, layer)
                v.scalar_tensor_tensor(out=wcol(0, layer, k * n, n), in0=staging[:, k * n:k * n + n], scalar=WS,
                                       in1=wcol(1, layer, k * n, n), op0=ALU.mult, op1=ALU.subtract).then_inc(w_lo_ok, 1)

            def moments(layer, b, st, mv, stat, mom, var):
                wait(ve, mom, layer, b, 0, apart=True)
                for t in range(NT):
                    last = v.bn_stats(st[:, t, :], tile_x(b, t))
                last.then_inc(stat.sem, 1)
                wait(ve, stat, layer, b, 1, apart=True)
                wait(ve, var, layer, b, 0, apart=True)
                for t in range(NT):
                    last = v.bn_aggr(mv[:, t, :], st[:, t, :])
                last.then_inc(mom.sem, 1)

            def normed(layer, b, xn, mv, r, rstd, done, turned):
                wait(ve, rstd, layer, b, 1)
                wait(ve, turned, layer, b, 0)
                for t in range(NT):
                    last = v.tensor_scalar(xn[:, t, :], tile_x(b, t), mv[:, t, 0:1], r[:, t:t + 1],
                                           ALU.subtract, ALU.mult)
                last.then_inc(done.sem, 1)

            def p_mask(layer, b, k):
                if layer == 3:
                    wait(ve, mask_in, layer, b, 16)
                    wait(ve, s_mul, layer, b, 0)
                    v.tensor_scalar(m_mul[:, :, :], m_raw[:, :, :], 0.0, None, ALU.not_equal).then_inc(mask_ok.sem, 1)

            def p_stats(layer, b, k):
                if layer:
                    wait(ve, x_mix, layer - 1, b, 1, apart=True)
                elif isinstance(b, int):
                    ve.wait_ge(in_x[min(b, 3)], 16)
                wait(ve, p_xn, layer, b, 0, apart=True)
                moments(layer, b, p_st, p_mv, p_stat, p_mom, p_var)

            def p_norm(layer, b, k):
                normed(layer, b, xn_a, p_mv, p_rs, p_rstd, p_xn, p_xT)

            def split(layer, b, bank, hl, col, hi, lo, in_dram):
                wait(ve, hi, layer, b, 1)
                wait(ve, in_dram, layer, b, 0)
                v.scalar_tensor_tensor(out=hl[:, 1, :], in0=bank[:, :], scalar=cols[:, col:col + 1], in1=hl[:, 0, :],
                                       op0=ALU.add, op1=ALU.subtract).then_inc(lo.sem, 1)

            def p_q(layer, b, k):
                split(layer, b, S[1], q_hl, 2 * layer, p_qh, p_ql, q_scr)

            def p_k(layer, b, k):
                split(layer, b, S[0], k_hl, 2 * layer + 1, p_kh, p_kl, k_scr)

            def p_v(layer, b, k):
                wait(ve, pv_ok, layer, b, 0)
                if layer == 0 and isinstance(b, int) and b == 0:
                    ve.wait_ge(c_pool, 3)
                bv = bc[:, layer * D:layer * D + D].rearrange("p (j h d) -> p j h d", j=8, h=2)
                for half in range(2):
                    wait(ve, p_vp, layer, b, half + 1)
                    src = S[half][:, :].rearrange("p (t b j h d) -> p t b j h d", t=2, b=2, j=8, h=2)
                    for h in range(2):
                        for e in range(2):
                            r = slice(64 * h, 64 * h + 64)
                            last = v.tensor_tensor(v_diag[r, 2 * half:2 * half + 2, :, e, h, 0:HD], src[r, :, e, :, h, :],
                                                   bv[r, :, h, :].unsqueeze(1).to_broadcast([64, 2, 8, HD]), ALU.add)
                last.then_inc(p_vd.sem, 1)

            def q_scores(layer, b, t):
                wait(ve, pt_ok, layer, b, 0)
                for half in range(2):
                    n = 2 * t + half + 1
                    s = S[half][:, :].rearrange("p (h k) -> p h k", h=8)
                    p = prob[:, t, half * 512:half * 512 + 512].rearrange("p (h k) -> p h k", h=8)
                    mx = q_mx[:, half, :]
                    wait(ve, s_ok, layer, b, n)
                    if layer == 3:
                        v.tensor_tensor(p, s, m_mul[:, t, :].unsqueeze(1).to_broadcast([128, 8, SEQ]), ALU.mult)\
                            .then_inc(s_mul.sem, 1)
                        wait(ve, s_mul, layer, b, n)
                        s = p
                    wait(ve, s_sub, layer, b, max(n - 2, 0))
                    v.tensor_reduce(mx, s, AX.X, ALU.max).then_inc(s_max.sem, 1)
                    wait(ve, s_max, layer, b, n)
                    if layer == 3:
                        v.scalar_tensor_tensor(out=p, in0=p, scalar=1e-20, in1=cast_row(mx, SEQ), op0=ALU.add,
                                               op1=ALU.subtract).then_inc(s_sub.sem, 1)
                    else:
                        v.tensor_tensor(p, s, cast_row(mx, SEQ), ALU.subtract).then_inc(s_sub.sem, 1)

            def q_turn_a(layer, b, t):
                wait(ve, pt_ok, layer, b, 2 * t + 1)
                wait(ve, pv_ok, layer, b, max(t - 1, 0))
                v.tensor_copy(probT[:, t % 2, 0:4, :].rearrange("p j n -> p (j n)"), T[:, :]).then_inc(pt_a.sem, 1)

            def q_pv(layer, b, t):
                wait(ve, pv_ok, layer, b, t + 1)
                wait(ve, o_ok, layer, b, t)
                a = A[:, 0:288].rearrange("p (j b h d) -> p j b h d", j=8, b=2, h=2)
                for e in range(2):
                    r = slice(64 * e, 64 * e + 64)
                    last = v.reciprocal(q_rc[r, :, :], a[r, :, e, :, HD])
                last.then_inc(rc_ok.sem, 1)
                wait(ve, rc_ok, layer, b, t + 1)
                wait(ve, ot_ok, layer, b, t)
                for e in range(2):
                    r = slice(64 * e, 64 * e + 64)
                    last = v.tensor_tensor(att[r, :].rearrange("p (j h d) -> p j h d", j=8, h=2), a[r, :, e, :, 0:HD],
                                           q_rc[r, :, :].unsqueeze(3).to_broadcast([64, 8, 2, HD]), ALU.mult)
                last.then_inc(o_ok.sem, 1)

            def q_out(layer, b, t):
                wait(ve, out_ok, layer, b, t + 1)
                x = tile_x(b, t)
                v.scalar_tensor_tensor(out=x, in0=A[:, 0:128], scalar=gate[:, layer:layer + 1], in1=x,
                                       op0=ALU.mult, op1=ALU.add).then_inc(x_att.sem, 1)

            def f_stats(layer, b, k):
                wait(ve, x_att, layer, b, 4, apart=True)
                wait(ve, f_xn, layer, b, 0, apart=True)
                moments(layer, b, f_st, f_mv, f_stat, f_mom, f_var)

            def f_norm(layer, b, k):
                normed(layer, b, xn_f, f_mv, f_rs, f_rstd, f_xn, f_xT)

            step = [0]

            def then(ins, layer, b, wait_apart=False):
                step[0] += 1
                ins.then_inc(rt.sem, 1)
                wait(ve, rt, layer, b, step[0], wait_apart)

            def f_logits(layer, b, k):
                E = EXPERTS[layer]
                lg, ex = r_lg[:, :, 0:E], r_ex[:, :, 0:E]
                step[0] = 0
                if layer != 1:
                    wait(ve, f_lg, layer, b, 1)
                    then(v.tensor_copy(lg, T[:, 0:NT * E].rearrange("p (t e) -> p t e", e=E)), layer, b)
                    then(v.tensor_reduce(r_s[:, 0, :], lg, AX.X, ALU.max), layer, b)
                    then(v.tensor_tensor(ex, lg, cast_row(r_s[:, 0, :], E), ALU.subtract), layer, b)

            def f_pick(layer, b, k):
                E = EXPERTS[layer]
                lg, ex, val = r_lg[:, :, 0:E], r_ex[:, :, 0:E], r_val[:, :, 0:E]
                oh, w, w2 = r_oh[:, :, :, 0:E], r_w[:, :, 0:E], r_w2[:, :, 0:E]
                wait(ve, rt_act, layer, b, 1, apart=layer == 0)
                if layer == 0:
                    val, key = ex, lg
                elif layer == 1:
                    then(v.tensor_scalar(val, lg, 0.5, 0.5, ALU.mult, ALU.add), layer, b, True)
                    key = val
                else:
                    then(v.tensor_reduce(r_s[:, 1, :], ex, AX.X, ALU.add), layer, b)
                    then(v.reciprocal(r_s[:, 2, :], r_s[:, 1, :]), layer, b)
                    then(v.tensor_tensor(val, ex, cast_row(r_s[:, 2, :], E), ALU.mult), layer, b, True)
                    key = val
                    if layer == 2:
                        key = r_key[:, :, 0:E]
                        gb = bc[:, 512:520].unsqueeze(1).to_broadcast([128, NT, E])
                        then(v.tensor_tensor(key, val, gb, ALU.add), layer, b, True)
                for t in range(NT):
                    last = v.max(r_top[:, t, :], key[:, t, :])
                then(last, layer, b, True)
                for t in range(NT):
                    last = v.max_index(r_idx[:, t, :], r_top[:, t, :], key[:, t, :])
                then(last, layer, b)
                then(v.tensor_copy(r_idf[:, :, :], r_idx[:, :, :]), layer, b)
                iota = cst[:, 344:344 + E].unsqueeze(1).to_broadcast([128, NT, E])
                v.tensor_tensor(oh[:, 0], iota, cast_row(r_idf[:, :, 0], E), ALU.is_equal)
                then(v.tensor_tensor(oh[:, 1], iota, cast_row(r_idf[:, :, 1], E), ALU.is_equal), layer, b)
                then(v.tensor_tensor(w, oh[:, 0], oh[:, 1], ALU.add), layer, b)
                then(v.tensor_tensor(w2, w, val, ALU.mult), layer, b)
                if layer != 2:
                    then(v.tensor_reduce(r_s[:, 3, :], w2, AX.X, ALU.add), layer, b)
                    if layer == 3:
                        then(v.tensor_scalar(r_s[:, 3, :], r_s[:, 3, :], 1e-9, None, ALU.max), layer, b)
                    then(v.reciprocal(r_s[:, 1, :], r_s[:, 3, :]), layer, b)
                    then(v.tensor_tensor(w, w2, cast_row(r_s[:, 1, :], E), ALU.mult), layer, b)
                if layer == 0:
                    then(v.tensor_scalar(r_one[:, :, :], w, 0.0, None, ALU.is_gt), layer, b)
                    then(v.tensor_reduce(r_sum[:, :], r_one[:, :, :].rearrange("p t e -> p e t"), AX.X, ALU.add), layer, b)

            def f_parts(layer, b, k):
                E = EXPERTS[layer]
                w = r_w2[:, :, 0:E] if layer == 2 else r_w[:, :, 0:E]
                if layer == 0:
                    taken = r_w2[:, :, 0:E]
                    wait(ve, cum_ok, layer, b, 1)
                    then(v.scalar_tensor_tensor(out=taken, in0=A[:, 0:NT * E].rearrange("p (t e) -> p t e", e=E),
                                                scalar=float(CAPACITY), in1=w, op0=ALU.is_le, op1=ALU.mult), layer, b)
                    then(v.tensor_tensor(carry[:, :], carry[:, :], r_sum[:, :], ALU.add), layer, b)
                    w = taken
                parts = w3[:, :, 0:3 * E].rearrange("p t (k e) -> p t k e", k=3)
                rest = r_rest[:, :, :, 0:E]
                wait(ve, wt_ok, layer, b, 0)
                then(v.tensor_copy(parts[:, :, 0, :], w), layer, b)
                then(v.tensor_tensor(rest[:, 0], w, parts[:, :, 0, :], ALU.subtract), layer, b)
                then(v.tensor_copy(parts[:, :, 1, :], rest[:, 0]), layer, b)
                then(v.tensor_tensor(rest[:, 1], rest[:, 0], parts[:, :, 1, :], ALU.subtract), layer, b)
                v.tensor_copy(parts[:, :, 2, :], rest[:, 1]).then_inc(w3_ok.sem, 1)
                assert step[0] == ROUTE_STEPS[layer]

            def m_start(layer, b, k):
                wait(ve, m_xh, layer, b, 1)
                wait(ve, filled, layer, b, 0)
                wait(ve, y_ok, layer, b, 0)
                v.tensor_tensor(x_lo[:, :], xnT_f[:, :], x_hi[:, :], ALU.subtract).then_inc(m_xl.sem, 1)

            def hw_free(layer, b, u):
                wait(ve, hi_ok, layer, b, max(u - 1, 0))
                wait(ve, lo_ok, layer, b, max(u - 1, 0))

            def m_unit(layer, b, u):
                if u < UNITS[layer]:
                    k = RING_OF[layer][u][-1]
                    bank = R[k % 3]
                    if layer == 0:
                        wait(ve, filled, layer, b, k + 1)
                        wait(ve, read_act, layer, b, u // 2 + 1)
                        hw_free(layer, b, u)
                        v.scalar_tensor_tensor(out=hw[:, u % 2, :], in0=bank[:, :], scalar=0.0,
                                               in1=w_bc[:, u // 2 % 2, :], op0=ALU.max, op1=ALU.mult).then_inc(read_dve.sem, 1)
                    elif layer in (1, 2):
                        pool = HW_POOL[layer]
                        m = 64 if layer == 1 and u == 8 else 128
                        wait(ve, filled, layer, b, k + 1)
                        wait(ve, read_act, layer, b, act_read(layer, k - 1))
                        if u < pool:
                            wait(ve, hw_pool, layer, b, max(u - 1, 0))
                            to = had
                        else:
                            wait(ve, hw_pool, layer, b, pool)
                            hw_free(layer, b, u)
                            to = hw
                        v.scalar_tensor_tensor(out=to[0:m, u % 2, :], in0=bank[0:m, :], scalar=1.0 / WS,
                                               in1=act[0:m, u % 2, :], op0=ALU.mult, op1=ALU.mult).then_inc(read_dve.sem, 1)
                    else:
                        k = RING_OF[3][u][0]
                        wait(ve, filled, layer, b, k + 1)
                        wait(ve, read_act, layer, b, u + 1)
                        wait(ve, gelu_ok, layer, b, max(u - 1, 0))
                        v.tensor_tensor(act[:, u % 2, :], hidden[:, u, :], R[k % 3][:, :], ALU.mult).then_inc(read_dve.sem, 1)
                u -= 1
                if not 0 <= u < UNITS[layer]:
                    return
                if layer == 3:
                    k = RING_OF[3][u][1]
                    wait(ve, filled, layer, b, k + 1)
                    wait(ve, gelu_ok, layer, b, u + 1)
                    hw_free(layer, b, u)
                    v.tensor_tensor(hw[:, u % 2, :], had[:, u % 2, :], R[k % 3][:, :], ALU.mult).then_inc(read_dve.sem, 1)
                elif layer in (1, 2):
                    lo_part(ve, layer, b, u)

            def m_mid(layer, b, k):
                wait(ve, sd_ok, layer, b, 1)
                wait(ve, filled, layer, b, 0)
                wait(ve, read_dve, layer, b, 0)
                sd, rs, rest = act[0:16, 0, :], act[0:16, 1, :], had[0:16, 0, :]
                part = had[0:16, 1, :].bitcast(BF16)[:, 0:BLK]
                steps_ = [lambda: v.reciprocal(rs, sd),
                          lambda: v.tensor_copy(rsT[0:16, :], rs),
                          lambda: v.tensor_tensor(rest, rs, rsT[0:16, :], ALU.subtract),
                          lambda: v.tensor_copy(part, rest),
                          lambda: v.tensor_copy(rsT[32:48, :], part),
                          lambda: v.tensor_tensor(rsT[64:80, :], rest, part, ALU.subtract)]
                for n, step in enumerate(steps_):
                    step().then_inc(rs_ok.sem, 1)
                    if n != 4:
                        wait(ve, rs_ok, layer, b, n + 1)

            def m_end(layer, b, k):
                n = len(RING[layer]) - 1
                wait(ve, filled, layer, b, n + 1)
                x = tile_x(b, 0, NT)
                v.scalar_tensor_tensor(out=x, in0=R[n % 3][:, :], scalar=gate_ffn[:, layer:layer + 1], in1=x,
                                       op0=ALU.mult, op1=ALU.add).then_inc(x_mix.sem, 1)

            walk("ve", ve, dict(w_split=w_split, p_mask=p_mask, p_stats=p_stats, p_norm=p_norm, p_q=p_q, p_k=p_k, p_v=p_v,
                          q_scores=q_scores, q_turn_a=q_turn_a, q_pv=q_pv, q_out=q_out, f_stats=f_stats, f_norm=f_norm,
                          f_logits=f_logits, f_pick=f_pick, f_parts=f_parts, m_start=m_start,
                          m_unit=m_unit, m_mid=m_mid, m_end=m_end), enter)

        @block.gpsimd
        def _(gp):
            g = nc.gpsimd
            g.memset(k_diag[:, :, :, :], 0.0).then_inc(c_pool, 1)
            g.memset(v_diag[:, :, :, :, :, :], 0.0).then_inc(c_pool, 1)
            gp.wait_ge(c_pool, 2)
            for h in range(2):
                last = g.memset(v_diag[64 * h:64 * h + 64, :, :, :, h, HD:HD + 1], 1.0)
            last.then_inc(c_pool, 1)
            gp.wait_ge(c_pool, 3)
            gp.wait_ge(c_dve, 1)

            def rstd(layer, b, mv, ve_, r, mom, var, out_, normed):
                wait(gp, mom, layer, b, 1, apart=True)
                wait(gp, out_, layer, b, 0, apart=True)
                g.tensor_scalar(ve_[:, :], mv[:, :, 1], EPS, None, ALU.add).then_inc(var.sem, 1)
                wait(gp, var, layer, b, 1)
                wait(gp, normed, layer, b, 0)
                g.tensor_tensor(r[:, :], ve_[:, :], neg_half[:, :], ALU.pow).then_inc(out_.sem, 1)

            def p_mask(layer, b, k):
                if layer in (0, 2):
                    wait(gp, mask_in, layer, b, 16 if layer == 0 else 32, apart=True)
                    wait(gp, s_ok, layer, b, 0, apart=True)
                    g.tensor_scalar(m_add[:, :, :], m_raw[:, :, :], 0.0, MASKED, ALU.is_equal, ALU.mult)\
                        .then_inc(mask_ok.sem, 1)

            def p_stats(layer, b, k):
                rstd(layer, b, p_mv, p_ve, p_rs, p_mom, p_var, p_rstd, p_xn)

            def f_stats(layer, b, k):
                rstd(layer, b, f_mv, f_ve, f_rs, f_mom, f_var, f_rstd, f_xn)

            def m_start(layer, b, k):
                n = 3 * EXPERTS[layer]
                wait(gp, wt_sv, layer, b, 1, apart=True)
                wait(gp, filled, layer, b, 0, apart=True)
                wait(gp, y_ok, layer, b, 0, apart=True)
                g.tensor_copy(wT[0:n, :], wT_next[0:n, :]).then_inc(m_wc.sem, 1)

            def m_pre(layer, b, e):
                if e < 16:
                    wait(gp, read_act, layer, b, e + 1)
                    if e < 2:
                        wait(gp, hi_ok, layer, b, 0)
                        wait(gp, lo_ok, layer, b, 0)
                    else:
                        wait(gp, var_ok, layer, b, e - 1)
                    g.tensor_tensor(hw[:, e % 2, :], hidden[:, e, :], hidden[:, e, :], ALU.mult).then_inc(sq_ok.sem, 1)

            def m_unit(layer, b, u):
                if layer in (1, 2) and u < HW_POOL[layer]:
                    e = u // 2 if layer == 2 else u
                    wait(gp, read_dve, layer, b, u + 1)
                    wait(gp, hi_ok, layer, b, max(u - 1, 0))
                    wait(gp, lo_ok, layer, b, max(u - 1, 0))
                    g.tensor_tensor(hw[:, u % 2, :], had[:, u % 2, :], w_bc[:, e % 2, :], ALU.mult).then_inc(hw_pool.sem, 1)
                u -= LATE[layer]
                if layer in (0, 3) and 0 <= u < UNITS[layer]:
                    lo_part(g, layer, b, u)

            walk("gp", gp, dict(p_mask=p_mask, p_stats=p_stats, f_stats=f_stats, m_start=m_start, m_pre=m_pre, m_unit=m_unit),
                 lambda layer: None)


def kernel(**inputs):
    import numpy as np
    import concourse.bacc as bacc
    from concourse.bass_utils import run_bass_kernel_spmd

    a = {k: np.asarray(x) for k, x in inputs.items()}
    f = np.float32

    def T(x):
        return np.ascontiguousarray(np.swapaxes(x, -1, -2))

    def flat(x):
        return np.transpose(x, (1, 0, 2)).reshape(x.shape[1], -1)

    def chunks(x):
        return np.transpose(x.reshape(x.shape[0], 2, 128, -1), (2, 0, 1, 3)).reshape(128, -1)

    att = [[T(a[f"L{i}_xattn_W{w}"]) for w in "qkvo"] for i in range(LAYERS)]
    w_att = flat(np.stack([w for layer in att for w in layer]))
    l1_down = a["L1_ffn_experts_wd"].reshape(8, 128, D)
    shared_down = np.concatenate([a["L1_ffn_shared_wd"], np.zeros((64, D), f)])
    l2 = {w: np.concatenate([a[f"L2_ffn_w{w}"], a[f"L2_ffn_sw{w}"][None]]) for w in "123"}
    w_moe = np.concatenate([
        flat(T(a["L0_ffn_first_linear"])), chunks(T(a["L0_ffn_second_linear"])),
        flat(a["L1_ffn_experts_wg"]), a["L1_ffn_shared_wg"], flat(a["L1_ffn_experts_wu"]), a["L1_ffn_shared_wu"],
        flat(l1_down), shared_down,
        flat(T(l2["1"])), flat(T(l2["3"])), chunks(T(l2["2"])),
        flat(a["L3_ffn_W1"]), flat(a["L3_ffn_W2"])], axis=1)
    w_rt = np.concatenate([T(a["L0_ffn_expert_embeddings"]), a["L1_ffn_gate_w"], T(a["L2_ffn_gate_w"]), a["L3_ffn_Wr"]], axis=1)
    rows = np.concatenate([a["L0_xattn_bo"], a["L2_xattn_bo"], a["L3_xattn_bo"], a["L1_ffn_gate_b"], a["L3_ffn_br"]])[None]
    none = np.zeros(D, f)
    cols = np.stack([none] * 4 + [a["L2_xattn_bq"], a["L2_xattn_bk"], a["L3_xattn_bq"], a["L3_xattn_bk"]], axis=1)
    cols = np.concatenate([cols, T(a["L3_ffn_g1"]), T(a["L3_ffn_be1"])], axis=1)
    bc = np.concatenate([none, none, a["L2_xattn_bv"], a["L3_xattn_bv"], a["L2_ffn_gate_bias"], a["g_xattn"], a["g_ffn"]])[None]
    causal = np.tile(np.where(np.tril(np.ones((SEQ, SEQ), bool)), 0.0, MASKED), (2, 1))
    row = np.arange(128)[:, None]
    cst = np.concatenate([np.eye(128), np.triu(np.ones((128, 128))), causal, row % 8 == np.arange(8)[None],
                          row % 16 == np.arange(16)[None], np.tile(np.arange(16), (128, 1)), row % 32 == np.arange(16)[None]], axis=1).astype(f)
    m2 = np.transpose(a["mask_BxS2_ik0"].reshape(NB, NT, 2, SEQ), (0, 2, 1, 3)).reshape(NB, 2, NT * SEQ)
    arrays = {
        "x": a["x"].reshape(TOK, D), "ctxT": T(a["ctx_1024"].reshape(TOK, D)),
        "m0": a["mask_Bx1xSxS2_if1"].reshape(TOK, SEQ), "m2": m2, "m3": a["mask_Bx1xSxS2_ik1"].reshape(TOK, SEQ),
        "w_att": w_att, "w_moe": w_moe, "w_rt": w_rt, "rows": rows, "cols": cols, "bc": bc,
        "b1": a["L3_ffn_b1"], "b2": np.concatenate([a["L3_ffn_b2"]] * 3), "cst": cst,
    }
    arrays = {f"{k}_dram": np.ascontiguousarray(x) for k, x in arrays.items()}
    nc = bacc.Bacc("TRN2", target_bir_lowering=False, num_devices=1, dynamic_dma_scratch_size=1024)
    args = [nc.dram_tensor(k, x.shape, mybir.dt.from_np(x.dtype), kind="ExternalInput").ap() for k, x in arrays.items()]
    out = nc.dram_tensor("out_dram", (TOK, D), F32, kind="ExternalOutput").ap()
    build(nc, *args, out)
    r = run_bass_kernel_spmd(nc, [arrays], core_ids=[0])
    return r.results[0]["out_dram"].reshape(BATCH, SEQ, D)
```
